# Optimizing a Trainium2 kernel written in Bass

```python
import numpy as np
import jax
import jax.numpy as jnp

def _softmax(x, axis=-1):
    return jax.nn.softmax(x, axis=axis)

def _gelu(x):
    return jax.nn.gelu(x, approximate=True)

def _silu(x):
    return jax.nn.silu(x)

def _sigmoid(x):
    return jax.nn.sigmoid(x)

def _layernorm(x, axis=-1, eps=1e-05):
    m = jnp.mean(x, axis=axis, keepdims=True)
    v = jnp.var(x, axis=axis, keepdims=True)
    return (x - m) / jnp.sqrt(v + eps)

def _scatter_add(tgt, idx, src, axis=0):
    return tgt.at[idx].add(src)

def _segment_sum(src, seg, n):
    return jax.ops.segment_sum(src, seg, n)
kernel_name = 'mk_gnn_preln_d4_gnn_r16_fb955f'

def setup_inputs(seed: int=0):
    np.random.seed(seed)
    _w = jnp.asarray

    def _rec_inputs():
        import jax
        import jax.numpy as jnp
        _gk = jax.random.key(seed)
        x = -0.0009044 + 1 * jax.random.normal(jax.random.fold_in(_gk, 1), (6250, 32), jnp.float32)
        src = jax.random.randint(jax.random.fold_in(_gk, 2), (200000,), 0, 6250, jnp.int32)
        dst = jnp.minimum((6250 * jax.random.uniform(jax.random.fold_in(_gk, 3), (200000,)) ** 2.0).astype(jnp.int32), 99999)
        _o = jnp.argsort(dst, stable=True)
        src = src[_o]
        dst = dst[_o]
        edge_attr_3 = -0.000451519 + 1.00018 * jax.random.normal(jax.random.fold_in(_gk, 12), (200000, 3), jnp.float32)
        edge_attr_32 = -9.77346e-05 + 0.999888 * jax.random.normal(jax.random.fold_in(_gk, 13), (200000, 32), jnp.float32)
        return (x, src, dst, edge_attr_3, edge_attr_32)
    x, src, dst, edge_attr_3, edge_attr_32 = _rec_inputs()

    def _L0_gnn_setup():
        import jax, jax.numpy as jnp
        import numpy as np

        def real_sh_l3(vec):
            r = jnp.sqrt(jnp.sum(vec * vec, axis=-1, keepdims=True))
            v = vec / jnp.maximum(r, jnp.asarray(1e-12, vec.dtype))
            x, y, z = (v[:, 0], v[:, 1], v[:, 2])
            x2, y2, z2 = (x * x, y * y, z * z)
            C0 = 0.28209479177387814
            C1 = 0.4886025119029199
            Y = [jnp.full_like(x, C0), C1 * y, C1 * z, C1 * x, 1.0925484305920792 * x * y, 1.0925484305920792 * y * z, 0.31539156525252005 * (3.0 * z2 - 1.0), 1.0925484305920792 * x * z, 0.5462742152960396 * (x2 - y2), 0.5900435899266435 * y * (3.0 * x2 - y2), 2.890611442640554 * x * y * z, 0.4570457994644658 * y * (5.0 * z2 - 1.0), 0.3731763325901154 * z * (5.0 * z2 - 3.0), 0.4570457994644658 * x * (5.0 * z2 - 1.0), 1.445305721320277 * z * (x2 - y2), 0.5900435899266435 * x * (x2 - 3.0 * y2)]
            return jnp.stack(Y, axis=-1)
        key = jax.random.key(seed)
        k1, k2, k3, k4, k5 = jax.random.split(key, 5)
        n_atoms, hidden, num_irreps, out_ch = (3125, 32, 16, 32)
        n_edges = 50000
        node_features = jax.random.normal(k1, (n_atoms, hidden), dtype=jnp.float32)
        edge_vectors = jax.random.normal(k2, (n_edges, 3), dtype=jnp.float32)
        edge_index = jax.random.randint(k3, (2, n_edges), 0, n_atoms, dtype=jnp.int64)
        fan_in = hidden * num_irreps
        W = jax.random.normal(k4, (fan_in, out_ch), dtype=jnp.float32) / np.sqrt(fan_in)
        b = jax.random.normal(k5, (out_ch,), dtype=jnp.float32) * 0.01
        return {'node_features': node_features, 'edge_vectors': edge_vectors, 'edge_index': edge_index, 'W': W, 'b': b}
    _L0_gnn_all = _L0_gnn_setup()
    _L0_gnn_in = {k: v for k, v in _L0_gnn_all.items() if k in ('W', 'b')}
    del _L0_gnn_all

    def _L1_gnn_setup():
        import jax, jax.numpy as jnp
        import numpy as np
        N_NODES = 3125
        DEG = 16
        N_HEAD = 4
        F_IN = 32
        F_OUT = 32
        key = jax.random.key(seed)
        k_h, k_w, k_fw, k_fb = jax.random.split(key, 4)
        h = jax.random.normal(k_h, (N_NODES, F_IN), dtype=jnp.float32)
        src = jnp.repeat(jnp.arange(N_NODES, dtype=jnp.int64), DEG)
        offs = (jnp.arange(DEG, dtype=jnp.int64) + 1) * 97
        dst = (src.reshape(N_NODES, DEG) + offs[None, :]).reshape(-1) % N_NODES
        edge_index = jnp.stack([src, dst], axis=0)
        gain = 1.414
        bound_w = gain * np.sqrt(6.0 / (F_IN + F_OUT))
        w = jax.random.uniform(k_w, (N_HEAD, F_IN, F_OUT), jnp.float32, -bound_w, bound_w)
        bound_fc = np.sqrt(1.0 / (2 * F_OUT))
        fc_w = jax.random.uniform(k_fw, (1, 2 * F_OUT), jnp.float32, -bound_fc, bound_fc)
        fc_b = jax.random.uniform(k_fb, (1,), jnp.float32, -bound_fc, bound_fc)
        bias = jnp.zeros((F_OUT,), jnp.float32)
        return {'h': h, 'edge_index': edge_index, 'w': w, 'fc_w': fc_w, 'fc_b': fc_b, 'bias': bias}
    _L1_gnn_all = _L1_gnn_setup()
    _L1_gnn_in = {k: v for k, v in _L1_gnn_all.items() if k in ('w', 'fc_w', 'fc_b', 'bias')}
    del _L1_gnn_all

    def _L2_gnn_setup():
        import jax, jax.numpy as jnp
        import numpy as np
        EPS_DENOM = 1e-07
        EPS_NORM = 1e-05

        def _fcnn(x, W1, b1, W2, b2):
            return jax.nn.relu(x @ W1 + b1) @ W2 + b2
        key = jax.random.key(seed)
        N, E, D, H = (6250, 100000, 32, 128)
        ks = jax.random.split(key, 11)
        node_features = jax.random.normal(ks[0], (N, D), jnp.float32)
        edge_features = jax.random.normal(ks[1], (E, D), jnp.float32)
        edge_index = jax.random.randint(ks[2], (2, E), 0, N, dtype=jnp.int64)
        sD = 1.0 / np.sqrt(D)
        sH = 1.0 / np.sqrt(H)
        W1a = jax.random.normal(ks[3], (D, H), jnp.float32) * sD
        b1a = jax.random.normal(ks[4], (H,), jnp.float32) * sD
        W2a = jax.random.normal(ks[5], (H, D), jnp.float32) * sH
        b2a = jax.random.normal(ks[6], (D,), jnp.float32) * sH
        W1b = jax.random.normal(ks[7], (D, H), jnp.float32) * sD
        b1b = jax.random.normal(ks[8], (H,), jnp.float32) * sD
        W2b = jax.random.normal(ks[9], (H, D), jnp.float32) * sH
        b2b = jax.random.normal(ks[10], (D,), jnp.float32) * sH
        return dict(node_features=node_features, edge_features=edge_features, W1a=W1a, b1a=b1a, W2a=W2a, b2a=b2a, W1b=W1b, b1b=b1b, W2b=W2b, b2b=b2b, edge_index=edge_index)
    _L2_gnn_all = _L2_gnn_setup()
    _L2_gnn_in = {k: v for k, v in _L2_gnn_all.items() if k in ('W1a', 'b1a', 'W2a', 'b2a', 'W1b', 'b1b', 'W2b', 'b2b')}
    del _L2_gnn_all

    def _L3_gnn_setup():
        import jax, jax.numpy as jnp
        import numpy as np
        N_NODES = 6250
        N_EDGES = 25000
        D = 32
        EH = 128
        STEPS = 6

        def _gru_cell(x, h, wih, whh, bih, bhh):
            gi = x @ wih.T + bih
            gh = h @ whh.T + bhh
            ir, iz, inn = jnp.split(gi, 3, axis=-1)
            hr, hz, hn = jnp.split(gh, 3, axis=-1)
            r = jax.nn.sigmoid(ir + hr)
            z = jax.nn.sigmoid(iz + hz)
            n = jnp.tanh(inn + r * hn)
            return (1.0 - z) * n + z * h
        key = jax.random.key(seed)
        ks = jax.random.split(key, 12)
        s = 0.05
        return {'n_feat': jax.random.normal(ks[0], (N_NODES, D), jnp.float32), 'e_feat': jax.random.normal(ks[1], (N_EDGES, D), jnp.float32), 'src': jax.random.randint(ks[2], (N_EDGES,), 0, N_NODES, jnp.int32), 'dst': jax.random.randint(ks[3], (N_EDGES,), 0, N_NODES, jnp.int32), 'lin0_w': jax.random.normal(ks[4], (D, D), jnp.float32) * s, 'lin0_b': jnp.zeros((D,), jnp.float32), 'en1_w': jax.random.normal(ks[5], (EH, D), jnp.float32) * s, 'en1_b': jnp.zeros((EH,), jnp.float32), 'en2_w': jax.random.normal(ks[6], (D * D, EH), jnp.float32) * s, 'en2_b': jnp.zeros((D * D,), jnp.float32), 'conv_bias': jnp.zeros((D,), jnp.float32), 'gru_wih': jax.random.normal(ks[7], (3 * D, D), jnp.float32) * s, 'gru_whh': jax.random.normal(ks[8], (3 * D, D), jnp.float32) * s, 'gru_bih': jnp.zeros((3 * D,), jnp.float32), 'gru_bhh': jnp.zeros((3 * D,), jnp.float32)}
    _L3_gnn_all = _L3_gnn_setup()
    _L3_gnn_in = {k: v for k, v in _L3_gnn_all.items() if k in ('lin0_w', 'lin0_b', 'en1_w', 'en1_b', 'en2_w', 'en2_b', 'conv_bias', 'gru_wih', 'gru_whh', 'gru_bih', 'gru_bhh')}
    del _L3_gnn_all
    return {'x': x, 'src': src, 'dst': dst, 'edge_attr_3': edge_attr_3, 'edge_attr_32': edge_attr_32, 'L0_gnn_W': _L0_gnn_in['W'], 'L0_gnn_b': _L0_gnn_in['b'], 'L1_gnn_w': _L1_gnn_in['w'], 'L1_gnn_fc_w': _L1_gnn_in['fc_w'], 'L1_gnn_fc_b': _L1_gnn_in['fc_b'], 'L1_gnn_bias': _L1_gnn_in['bias'], 'L2_gnn_W1a': _L2_gnn_in['W1a'], 'L2_gnn_b1a': _L2_gnn_in['b1a'], 'L2_gnn_W2a': _L2_gnn_in['W2a'], 'L2_gnn_b2a': _L2_gnn_in['b2a'], 'L2_gnn_W1b': _L2_gnn_in['W1b'], 'L2_gnn_b1b': _L2_gnn_in['b1b'], 'L2_gnn_W2b': _L2_gnn_in['W2b'], 'L2_gnn_b2b': _L2_gnn_in['b2b'], 'L3_gnn_lin0_w': _L3_gnn_in['lin0_w'], 'L3_gnn_lin0_b': _L3_gnn_in['lin0_b'], 'L3_gnn_en1_w': _L3_gnn_in['en1_w'], 'L3_gnn_en1_b': _L3_gnn_in['en1_b'], 'L3_gnn_en2_w': _L3_gnn_in['en2_w'], 'L3_gnn_en2_b': _L3_gnn_in['en2_b'], 'L3_gnn_conv_bias': _L3_gnn_in['conv_bias'], 'L3_gnn_gru_wih': _L3_gnn_in['gru_wih'], 'L3_gnn_gru_whh': _L3_gnn_in['gru_whh'], 'L3_gnn_gru_bih': _L3_gnn_in['gru_bih'], 'L3_gnn_gru_bhh': _L3_gnn_in['gru_bhh']}

def reference(x, src, dst, edge_attr_3, edge_attr_32, L0_gnn_W, L0_gnn_b, L1_gnn_w, L1_gnn_fc_w, L1_gnn_fc_b, L1_gnn_bias, L2_gnn_W1a, L2_gnn_b1a, L2_gnn_W2a, L2_gnn_b2a, L2_gnn_W1b, L2_gnn_b1b, L2_gnn_W2b, L2_gnn_b2b, L3_gnn_lin0_w, L3_gnn_lin0_b, L3_gnn_en1_w, L3_gnn_en1_b, L3_gnn_en2_w, L3_gnn_en2_b, L3_gnn_conv_bias, L3_gnn_gru_wih, L3_gnn_gru_whh, L3_gnn_gru_bih, L3_gnn_gru_bhh):
    import jax
    import jax.numpy as jnp

    def _L0_gnn_ref(node_features, edge_vectors, edge_index, W, b):
        import jax, jax.numpy as jnp
        import numpy as np

        def real_sh_l3(vec):
            r = jnp.sqrt(jnp.sum(vec * vec, axis=-1, keepdims=True))
            v = vec / jnp.maximum(r, jnp.asarray(1e-12, vec.dtype))
            x, y, z = (v[:, 0], v[:, 1], v[:, 2])
            x2, y2, z2 = (x * x, y * y, z * z)
            C0 = 0.28209479177387814
            C1 = 0.4886025119029199
            Y = [jnp.full_like(x, C0), C1 * y, C1 * z, C1 * x, 1.0925484305920792 * x * y, 1.0925484305920792 * y * z, 0.31539156525252005 * (3.0 * z2 - 1.0), 1.0925484305920792 * x * z, 0.5462742152960396 * (x2 - y2), 0.5900435899266435 * y * (3.0 * x2 - y2), 2.890611442640554 * x * y * z, 0.4570457994644658 * y * (5.0 * z2 - 1.0), 0.3731763325901154 * z * (5.0 * z2 - 3.0), 0.4570457994644658 * x * (5.0 * z2 - 1.0), 1.445305721320277 * z * (x2 - y2), 0.5900435899266435 * x * (x2 - 3.0 * y2)]
            return jnp.stack(Y, axis=-1)
        n_atoms = node_features.shape[0]
        sources, targets = (edge_index[0], edge_index[1])
        Y = real_sh_l3(edge_vectors)
        msg = node_features[sources][:, :, None] * Y[:, None, :]
        agg = jax.ops.segment_sum(msg, targets, num_segments=n_atoms)
        out = agg.reshape(n_atoms, -1) @ W + b
        return out

    def _L1_gnn_ref(h, edge_index, w, fc_w, fc_b, bias):
        import jax, jax.numpy as jnp
        import numpy as np
        N_NODES = 3125
        DEG = 16
        N_HEAD = 4
        F_IN = 32
        F_OUT = 32
        n_head, f_in, f_out = w.shape
        n = h.shape[0]
        src, dst = (edge_index[0], edge_index[1])
        hp = jnp.einsum('nf,hfo->hno', h, w)
        w_src = fc_w[0, :f_out]
        w_dst = fc_w[0, f_out:]
        a_src = jnp.einsum('hnf,f->hn', hp, w_src)
        a_dst = jnp.einsum('hnf,f->hn', hp, w_dst)
        e = a_src[:, src] + a_dst[:, dst] + fc_b[0]
        e = jax.nn.leaky_relu(e, negative_slope=0.2)
        seg_max = jax.ops.segment_max(e.T, src, num_segments=n)
        e = jnp.exp(e - seg_max.T[:, src])
        seg_sum = jax.ops.segment_sum(e.T, src, num_segments=n)
        att = e / seg_sum.T[:, src]
        msg = att[:, :, None] * hp[:, dst, :]
        agg = jax.vmap(lambda m: jax.ops.segment_sum(m, src, num_segments=n))(msg)
        out = agg.mean(axis=0) + bias
        return out

    def _L2_gnn_ref(node_features, edge_features, W1a, b1a, W2a, b2a, W1b, b1b, W2b, b2b, edge_index):
        import jax, jax.numpy as jnp
        import numpy as np
        EPS_DENOM = 1e-07
        EPS_NORM = 1e-05

        def _fcnn(x, W1, b1, W2, b2):
            return jax.nn.relu(x @ W1 + b1) @ W2 + b2
        x = node_features
        N = x.shape[0]
        h1 = _fcnn(x, W1a, b1a, W2a, b2a)
        h2 = _fcnn(x, W1b, b1b, W2b, b2b)
        s = jax.nn.sigmoid(edge_features)
        seg = jnp.concatenate([edge_index[0], edge_index[1]])
        nbr = jnp.concatenate([edge_index[1], edge_index[0]])
        s2 = jnp.concatenate([s, s], axis=0)
        denom = EPS_DENOM + jax.ops.segment_sum(s2, seg, num_segments=N)
        msg = s2 / denom[seg] * h2[nbr]
        agg = jax.ops.segment_sum(msg, seg, num_segments=N)
        h = h1 + agg
        mu = jnp.mean(h, axis=-1, keepdims=True)
        var = jnp.var(h, axis=-1, keepdims=True)
        hn = (h - mu) * jax.lax.rsqrt(var + EPS_NORM)
        return x + jax.nn.relu(hn)

    def _L3_gnn_ref(n_feat, e_feat, src, dst, lin0_w, lin0_b, en1_w, en1_b, en2_w, en2_b, conv_bias, gru_wih, gru_whh, gru_bih, gru_bhh):
        import jax, jax.numpy as jnp
        import numpy as np
        N_NODES = 6250
        N_EDGES = 25000
        D = 32
        EH = 128
        STEPS = 6

        def _gru_cell(x, h, wih, whh, bih, bhh):
            gi = x @ wih.T + bih
            gh = h @ whh.T + bhh
            ir, iz, inn = jnp.split(gi, 3, axis=-1)
            hr, hz, hn = jnp.split(gh, 3, axis=-1)
            r = jax.nn.sigmoid(ir + hr)
            z = jax.nn.sigmoid(iz + hz)
            n = jnp.tanh(inn + r * hn)
            return (1.0 - z) * n + z * h
        n_nodes = n_feat.shape[0]
        out = jax.nn.relu(n_feat @ lin0_w.T + lin0_b)
        h = out
        eh = jax.nn.relu(e_feat @ en1_w.T + en1_b)
        w_e = (eh @ en2_w.T + en2_b).reshape(-1, D, D)
        for _ in range(STEPS):
            msg = jnp.einsum('ei,eio->eo', out[src], w_e)
            agg = jax.ops.segment_sum(msg, dst, num_segments=n_nodes) + conv_bias
            m = jax.nn.relu(agg)
            h = _gru_cell(m, h, gru_wih, gru_whh, gru_bih, gru_bhh)
            out = h
        return out
    edge_index = jnp.stack([src, dst])
    h = jnp.maximum(_layernorm(x, axis=-1), 0.0)
    x = x + _L0_gnn_ref(h, edge_attr_3, edge_index, L0_gnn_W, L0_gnn_b)
    h = jnp.maximum(_layernorm(x, axis=-1), 0.0)
    x = x + _L1_gnn_ref(h, edge_index, L1_gnn_w, L1_gnn_fc_w, L1_gnn_fc_b, L1_gnn_bias)
    h = jnp.maximum(_layernorm(x, axis=-1), 0.0)
    x = x + _L2_gnn_ref(h, edge_attr_32, L2_gnn_W1a, L2_gnn_b1a, L2_gnn_W2a, L2_gnn_b2a, L2_gnn_W1b, L2_gnn_b1b, L2_gnn_W2b, L2_gnn_b2b, edge_index)
    h = jnp.maximum(_layernorm(x, axis=-1), 0.0)
    x = x + _L3_gnn_ref(h, edge_attr_32, src, dst, L3_gnn_lin0_w, L3_gnn_lin0_b, L3_gnn_en1_w, L3_gnn_en1_b, L3_gnn_en2_w, L3_gnn_en2_b, L3_gnn_conv_bias, L3_gnn_gru_wih, L3_gnn_gru_whh, L3_gnn_gru_bih, L3_gnn_gru_bhh)
    return x

_drawn_inputs = setup_inputs


def setup_inputs(seed=0):
    import zlib

    import numpy as np

    out = dict(_drawn_inputs(seed))
    spreads = {'L1_gnn_bias': (0.0, 0.1),
     'L3_gnn_lin0_b': (0.0, 0.1),
     'L3_gnn_en1_b': (0.0, 0.1),
     'L3_gnn_en2_b': (0.0, 0.1),
     'L3_gnn_conv_bias': (0.0, 0.1),
     'L3_gnn_gru_bih': (0.0, 0.1),
     'L3_gnn_gru_bhh': (0.0, 0.1)}
    factors = {'L0_gnn_b': 8.0, 'L1_gnn_fc_w': 3.331}
    for name, (base, spread) in spreads.items():
        noise = np.random.default_rng([zlib.crc32(name.encode()), seed]).standard_normal(out[name].shape)
        drawn = base * np.exp(spread * noise) if base else spread * noise
        out[name] = jnp.asarray(drawn.astype(out[name].dtype))
    for name, factor in factors.items():
        out[name] = (out[name] * factor).astype(out[name].dtype)
    return out
```

```python
import concourse.bass as bass
from concourse import mybir
from contextlib import ExitStack

F32 = mybir.dt.float32
I32 = mybir.dt.int32
ALU = mybir.AluOpType
ACT = mybir.ActivationFunctionType
AXX = mybir.AxisListType.X

P = 128
D = 32
ROW = 40
W_SRC, W_DST, W_SLO, W_DLO, W_A3, W_A32 = 0, 1, 2, 3, 4, 7
NY = 16
HEADS = 4
EH = 128
STEPS = 6
U = 4
Q = 4


class Kit:
    pass


class Steps:

    def __init__(self, engine, sem, base=0):
        self.engine, self.sem, self.base, self.n = engine, sem, base, 0

    def __call__(self, instruction):
        self.n += 1
        instruction.then_inc(self.sem, 1)
        self.engine.wait_ge(self.sem, self.base + self.n)

    def turn(self, i, each):
        return Steps(self.engine, self.sem, self.base + self.n + i * each)

    def skip(self, count):
        self.n += count


def shapes(n_nodes, n_edges):
    k = Kit()
    k.N, k.E = n_nodes, n_edges
    k.NB = (k.N + P - 1) // P
    k.NP = k.NB * P
    k.LASTN = k.N - (k.NB - 1) * P
    k.G = 7
    k.NG = k.NB // k.G
    assert k.NG * k.G == k.NB
    k.TC = k.E // P
    k.REM = k.E - k.TC * P
    body = U * Q
    need = (k.E + k.NB * (P - 1)) // P
    k.NT = (need + body - 1) // body * body
    k.TURNS = k.NT // body
    k.BC = (k.NT + P - 1) // P
    return k


def semaphores(k, ctx, prefix=""):
    def make(name):
        handle = ctx.enter_context(k.nc.semaphore(prefix + name))
        ctx.callback(k.nc.gpsimd.sem_clear, handle)
        return handle
    return make


def rows_of(ap, p=P):
    return ap.rearrange("(b p) f -> p b f", p=p)


def spread(vector, parts=P):
    return vector.rearrange("(a f) -> a f", a=1).to_broadcast([parts, vector.shape[0]])


def column(vector):
    return vector.rearrange("(p a) -> p a", a=1)


def zero_psum(k, flat, banks, done):
    for b in range(banks):
        last = k.nc.tensor.matmul(flat[:, b * 512:(b + 1) * 512], k.zeros[:, 0:P], k.zeros[:, :],
                                  start=True, stop=True)
    last.then_inc(done, 1)


def layernorm_relu(k, step, x, h, big, small, squares_summed, scaled):
    v = k.nc.vector
    wide = [P, k.NB, D]
    step(v.tensor_reduce(small[:, 0, :], x[:, :, :], AXX, ALU.add))
    step(v.tensor_scalar(small[:, 0, :], small[:, 0, :], 1.0 / D, None, ALU.mult))
    step(v.tensor_tensor(h[:, :, :], x[:, :, :], small[:, 0, :].unsqueeze(2).to_broadcast(wide), ALU.subtract))
    step(v.tensor_tensor(big[:, :, :], h[:, :, :], h[:, :, :], ALU.mult))
    step(v.tensor_reduce(small[:, 1, :], big[:, :, :], AXX, ALU.add))
    v.tensor_scalar(small[:, 1, :], small[:, 1, :], 1.0 / D, 1e-5, ALU.mult, ALU.add).then_inc(squares_summed, 1)
    step.engine.wait_ge(scaled, 1)
    step(v.reciprocal(small[:, 1, :], small[:, 1, :]))
    step(v.tensor_tensor(h[:, :, :], h[:, :, :], small[:, 1, :].unsqueeze(2).to_broadcast(wide), ALU.mult))
    step(v.tensor_scalar(h[:, :, :], h[:, :, :], 0.0, None, ALU.max))


def layernorm_root(k, act, small, squares_summed, scaled):
    act.wait_ge(squares_summed, 1)
    k.nc.scalar.activation(small[:, 1, :], small[:, 1, :], ACT.Sqrt).then_inc(scaled, 1)


def load_and_prepare(k, a):
    nc = k.nc
    with ExitStack() as ctx:
        sb = lambda n, s, d=F32: ctx.enter_context(nc.sbuf_tensor(n, s, d))
        sem = semaphores(k, ctx)
        en1_rows = sb("en1_rows", [EH, D])
        en2_rows = sb("en2_rows", [P, D * D // P, EH])
        gru_rows = sb("gru_rows", [3 * D, 2, D])
        lin_rows = sb("lin_rows", [D, D])
        w0_rows = sb("w0_rows", [D, NY, D])
        gru_b = sb("gru_b", [P, 2, 3 * D])
        pad = sb("pad", [P, k.NT // Q // Q, ROW])
        big = sb("ln_big0", [P, k.NB, D])
        small = sb("ln_small0", [P, 2, k.NB])
        fc = sb("fc", [D, 2 * D])
        w1_rows = sb("w1_rows", [D, HEADS, D])
        w1_fc = sb("w1_fc", [D, HEADS, D])
        tp = ctx.enter_context(nc.psum_tensor("prep_tp", [P, 4, 512], F32))
        x_cleared, loaded, consts = sem("x_cleared"), sem("loaded"), sem("consts")
        pad_made, padded, turned, steps = sem("pad_made"), sem("padded"), sem("turned"), sem("prep_steps")
        squares_summed, scaled = sem("squares_summed0"), sem("scaled0")
        block = ctx.enter_context(nc.Block())
        n_loads = [0]

        @block.sync
        def _(sp):
            def load(out, in_):
                sp.dma_start(out, in_).then_inc(loaded, 16)
                n_loads[0] += 1
            load(en1_rows[:, :], a["L3_gnn_en1_w"])
            load(en2_rows[:, :, :], rows_of(a["L3_gnn_en2_w"]))
            load(gru_rows[:, 0, :], a["L3_gnn_gru_wih"])
            load(gru_rows[:, 1, :], a["L3_gnn_gru_whh"])
            load(lin_rows[:, :], a["L3_gnn_lin0_w"])
            load(w0_rows[:, :, :], a["L0_gnn_W"].rearrange("(i j) o -> i j o", i=D))
            load(gru_b[:, 0, :], spread(a["L3_gnn_gru_bih"]))
            load(gru_b[:, 1, :], spread(a["L3_gnn_gru_bhh"]))
            load(fc[:, :], a["L1_gnn_fc_w"].to_broadcast([D, 2 * D]))
            load(w1_rows[:, :, :], a["L1_gnn_w"].rearrange("h f o -> f h o"))
            load(k.b0[:, :], spread(a["L0_gnn_b"]))
            load(k.w1[:, :], a["L1_gnn_w"].rearrange("h f o -> (h f) o"))
            load(k.fcb[:, :], spread(a["L1_gnn_fc_b"]))
            load(k.b1[:, :], spread(a["L1_gnn_bias"]))
            for n, s in enumerate("ab"):
                load(k.w2in[:, n, :], a[f"L2_gnn_W1{s}"])
                load(k.b2in[:, n:n + 1], column(a[f"L2_gnn_b1{s}"]))
                load(k.w2out[:, n, :], a[f"L2_gnn_W2{s}"])
                load(k.b2out[:, n, :], spread(a[f"L2_gnn_b2{s}"]))
            load(k.lin_b[:, :], spread(a["L3_gnn_lin0_b"]))
            load(k.en1_b[:, :], column(a["L3_gnn_en1_b"]))
            load(k.en2_b[:, :], a["L3_gnn_en2_b"].rearrange("(i o) -> i o", i=D))
            load(k.conv_b[:, :], spread(a["L3_gnn_conv_bias"]))
            sp.wait_ge(x_cleared, 1)
            load(k.X[:, 0:k.NB - 1, :], rows_of(a["x"][0:(k.NB - 1) * P, :]))
            load(k.X[0:k.LASTN, k.NB - 1, :], a["x"][(k.NB - 1) * P:k.N, :])

        @block.scalar
        def _(act):
            layernorm_root(k, act, small, squares_summed, scaled)
            act.wait_ge(pad_made, 3)
            n = Q * Q
            for s in range(2):
                view = k.edges[s].rearrange("(p c t) w -> p c (t w)", p=P, c=n)
                for c in range(n):
                    act.dma_start(view[:, c, :], pad[:, :, :].rearrange("p t w -> p (t w)")).then_inc(padded, 16)
            act.wait_ge(padded, 2 * n * 16)

        @block.gpsimd
        def _(pool):
            step = Steps(pool, pad_made)
            step(nc.gpsimd.memset(pad[:, :, :], 0.0))
            step(nc.gpsimd.memset(pad[:, :, W_SLO:W_DLO + 1], -1.0))
            step(nc.gpsimd.memset(k.zeros[:, :], 0.0))
            step = Steps(pool, consts)
            step(nc.gpsimd.iota(k.iota[:, :], [[1, P]], base=0, channel_multiplier=0,
                                allow_small_or_imprecise_dtypes=True))
            step(nc.gpsimd.memset(k.ident[:, :], 0.0))
            step(nc.gpsimd.memset(k.ones[:, :], 1.0))
            step(nc.gpsimd.affine_select(out=k.ident[:, :], in_=k.ident[:, :], compare_op=ALU.not_equal,
                                         fill=1.0, base=0, pattern=[[-1, P]], channel_multiplier=1))
            step(nc.gpsimd.affine_select(out=k.below[:, :], in_=k.ones[:, :], compare_op=ALU.is_gt,
                                         fill=0.0, base=0, pattern=[[1, P]], channel_multiplier=-1))

        @block.tensor
        def _(pe):
            pe.wait_ge(consts, 5)
            pe.wait_ge(loaded, 16 * n_loads[0])
            flip = nc.tensor.transpose
            for c in range(8):
                flip(tp[:, c // 4, c % 4 * P:c % 4 * P + P], en2_rows[:, c, :], k.ident[:, :])
            flip(tp[0:D, 2, 0:EH], en1_rows[:, :], k.ident[:, :])
            for s in range(2):
                flip(tp[0:D, 2, P + s * 96:P + s * 96 + 96], gru_rows[:, s, :], k.ident[0:96, 0:96])
            flip(tp[0:D, 3, 0:D], lin_rows[:, :], k.ident[0:D, 0:D]).then_inc(turned, 1)

        @block.vector
        def _(dve):
            v = nc.vector
            step = Steps(dve, steps)
            step(v.memset(k.X[:, k.NB - 1, :], 0.0))
            v.memset(k.rgru[:, :], 0.0).then_inc(x_cleared, 1)
            dve.wait_ge(loaded, 16 * n_loads[0])
            step(v.tensor_copy(k.w0[:, :].rearrange("i (o j) -> i j o", j=NY), w0_rows[:, :, :]))
            for s in range(2):
                step(v.tensor_tensor(w1_fc[:, :, :], w1_rows[:, :, :],
                                     fc[:, s * D:s * D + D].unsqueeze(1).to_broadcast([D, HEADS, D]), ALU.mult))
                step(v.tensor_reduce(k.wa[:, s * HEADS:(s + 1) * HEADS], w1_fc[:, :, :], AXX, ALU.add))
            step(v.tensor_tensor(k.gate_b[:, 0:2 * D], gru_b[:, 0, 0:2 * D], gru_b[:, 1, 0:2 * D], ALU.add))
            step(v.tensor_copy(k.gate_b[:, 2 * D:4 * D].rearrange("p (s f) -> p s f", s=2), gru_b[:, :, 2 * D:3 * D]))
            layernorm_relu(k, step, k.X, k.H, big, small, squares_summed, scaled)
            dve.wait_ge(turned, 1)
            for c in range(8):
                step(v.tensor_copy(
                    k.w2[:, :].rearrange("k (o i) -> k i o", i=D)[:, 4 * c:4 * c + 4, :],
                    tp[:, c // 4, c % 4 * P:c % 4 * P + P].rearrange("k (i o) -> k i o", i=4)))
            step(v.tensor_copy(k.en1[:, :], tp[0:D, 2, 0:EH]))
            step(v.tensor_copy(k.rgru[0:D, 0:3 * D], tp[0:D, 2, P:P + 96]))
            step(v.tensor_copy(k.rgru[D:2 * D, 0:2 * D], tp[0:D, 2, P + 96:P + 96 + 2 * D]))
            step(v.tensor_copy(k.rgru[D:2 * D, 3 * D:4 * D], tp[0:D, 2, P + 96 + 2 * D:P + 192]))
            step(v.tensor_copy(k.lin[:, :], tp[0:D, 3, 0:D]))


def place_edges(k, a):
    nc = k.nc
    T1 = k.TC + 1
    with ExitStack() as ctx:
        sb = lambda n, s, d=F32: ctx.enter_context(nc.sbuf_tensor(n, s, d))
        sem = semaphores(k, ctx)
        keys = sb("keys", [P, 2, T1], I32)
        part = sb("part", [P, T1], I32)
        hi = sb("hi", [P, 2, T1])
        mask = sb("mask", [P, 2, T1])
        rank = sb("rank", [P, T1])
        picked = sb("picked", [P, T1])
        count = sb("count", [P, 2, k.NB])
        tiles_i = sb("tiles_i", [P, 2, k.NB], I32)
        tiles = sb("tiles", [P, 2, k.NB])
        last = sb("last", [P, 2, k.NB])
        start = sb("start", [P, 2, k.NB])
        tile_no = sb("tile_no", [P, k.BC])
        ended = sb("ended", [P, k.BC, k.NB])
        of_tile = sb("of_tile", [P, k.BC])
        of_tile_i = sb("of_tile_i", [P, 2, k.BC], I32)
        sums = ctx.enter_context(nc.psum_tensor("count_sums", [P, 2, 2, P], F32))
        loaded, cleared, counted, summed = sem("keys_in"), sem("keys_cleared"), sem("counted"), sem("summed")
        steps, numbered, table, tabled = sem("place_steps"), sem("numbered"), sem("table"), sem("tabled")
        block = ctx.enter_context(nc.Block())

        @block.sync
        def _(sp):
            sp.wait_ge(cleared, 1)
            for s, name in enumerate(("src", "dst")):
                sp.dma_start(keys[:, s, 0:k.TC], a[name][0:k.TC * P].rearrange("(p t) -> p t", p=P)).then_inc(loaded, 16)
                sp.dma_start(keys[0:k.REM, s, k.TC:T1], column(a[name][k.TC * P:k.E])).then_inc(loaded, 16)
            sp.wait_ge(table, 1)
            with nc.allow_non_contiguous_dma(reason="a small table is turned"):
                sp.dma_start(k.block_dram[:, :].rearrange("s (c p) -> p s c", p=P), of_tile_i[:, :, :]).then_inc(tabled, 16)
            sp.wait_ge(tabled, 16)
            sp.dma_start(k.tile_block[0:1, :, U:U + k.BC * P], k.block_dram.rearrange("(a s) t -> a s t", a=1)).then_inc(tabled, 16)
            sp.wait_ge(tabled, 32)

        @block.gpsimd
        def _(pool):
            step = Steps(pool, numbered)
            step(nc.gpsimd.iota(tile_no[:, :], [[P, k.BC]], base=0, channel_multiplier=1,
                                allow_small_or_imprecise_dtypes=True))

        @block.tensor
        def _(pe):
            pe.wait_ge(counted, 1)
            for s in range(2):
                nc.tensor.matmul(sums[:, s, 0, 0:k.NB], k.ones[:, :], count[:, s, :], start=True, stop=True)
                done = nc.tensor.matmul(sums[:, s, 1, 0:k.NB], k.below[:, :], count[:, s, :], start=True, stop=True)
            done.then_inc(summed, 1)

        @block.vector
        def _(dve):
            v = nc.vector
            step = Steps(dve, steps)
            step(v.memset(k.tile_block[0:1, :, 0:U], 0))
            v.memset(keys[:, :, k.TC:T1], k.NB * P).then_inc(cleared, 1)
            dve.wait_ge(loaded, 64)
            for s in range(2):
                step(v.tensor_scalar(part[:, :], keys[:, s, :], 7, None, ALU.logical_shift_right))
                step(v.tensor_copy(hi[:, s, :], part[:, :]))
                step(v.tensor_copy(k.words[:, :, s], keys[:, s, :]))
                step(v.tensor_scalar(part[:, :], keys[:, s, :], P - 1, None, ALU.bitwise_and))
                step(v.tensor_copy(k.words[:, :, 2 + s], part[:, :]))
            with dve.Fori(0, k.NB) as b:
                turn = step.turn(b, 4)
                for s in range(2):
                    turn(v.tensor_scalar(mask[:, s, :], hi[:, s, :], k.iota[:, bass.ds(b, 1)], None, ALU.is_equal))
                    turn(v.tensor_reduce(count[:, s, bass.ds(b, 1)], mask[:, s, :], AXX, ALU.add))
            step.skip(4 * k.NB)
            dve.sem_inc(counted, 1)
            dve.wait_ge(summed, 1)
            dve.wait_ge(numbered, 1)
            for s in range(2):
                step(v.tensor_scalar(tiles[:, s, :], sums[:, s, 0, 0:k.NB], float(P - 1), None, ALU.add))
                step(v.tensor_copy(tiles_i[:, s, :], tiles[:, s, :]))
                step(v.tensor_scalar(tiles_i[:, s, :], tiles_i[:, s, :], 7, None, ALU.logical_shift_right))
                step(v.tensor_copy(tiles[:, s, :], tiles_i[:, s, :]))
                step(v.tensor_tensor_scan(last[:, s, :], k.ones[:, 0:k.NB], tiles[:, s, :], 0.0, ALU.mult, ALU.add))
                step(v.tensor_tensor(start[:, s, :], last[:, s, :], tiles[:, s, :], ALU.subtract))
                step(v.tensor_scalar(start[:, s, :], start[:, s, :], float(P), -1.0, ALU.mult, ALU.add))
                step(v.tensor_tensor(start[:, s, :], start[:, s, :], sums[:, s, 1, 0:k.NB], ALU.add))
                wide = [P, k.BC, k.NB]
                step(v.tensor_tensor(ended[:, :, :], last[:, s, :].unsqueeze(1).to_broadcast(wide),
                                     tile_no[:, :].unsqueeze(2).to_broadcast(wide), ALU.is_le))
                step(v.tensor_reduce(of_tile[:, :], ended[:, :, :], AXX, ALU.add))
                step(v.tensor_scalar(of_tile[:, :], of_tile[:, :], float(k.NB - 1), None, ALU.min))
                step(v.tensor_copy(of_tile_i[:, s, :], of_tile[:, :]))
            dve.sem_inc(table, 1)
            for s in range(2):
                step(v.memset(rank[:, :], 0.0))
                with dve.Fori(0, k.NB) as b:
                    turn = step.turn(b, 4)
                    turn(v.tensor_scalar(mask[:, 0, :], hi[:, s, :], k.iota[:, bass.ds(b, 1)], None, ALU.is_equal))
                    turn(v.tensor_tensor_scan(mask[:, 1, :], k.ones[:, 0:1].to_broadcast([P, T1]), mask[:, 0, :],
                                              start[:, s, bass.ds(b, 1)], ALU.mult, ALU.add))
                    turn(v.tensor_tensor(picked[:, :], mask[:, 0, :], mask[:, 1, :], ALU.mult))
                    turn(v.tensor_tensor(rank[:, :], rank[:, :], picked[:, :], ALU.add))
                step.skip(4 * k.NB)
                step(v.tensor_copy(part[:, :], rank[:, :]))
                step(v.tensor_scalar(keys[:, 0, :], part[:, :], P - 1, None, ALU.bitwise_and))
                step(v.tensor_scalar(part[:, :], part[:, :], 7, None, ALU.logical_shift_right))
                step(v.tensor_copy(rank[:, :], keys[:, 0, :]))
                step(v.tensor_copy(picked[:, :], part[:, :]))
                step(v.scalar_tensor_tensor(rank[:, :], rank[:, :], float(k.NT), picked[:, :], ALU.mult, ALU.add))
                step(v.tensor_copy(k.place[:, s, :], rank[:, :]))


def sort_edges(k, a):
    nc = k.nc
    C = 11
    turns = k.TC // (2 * C)
    assert turns * 2 * C == k.TC
    with ExitStack() as ctx:
        sb = lambda n, s, d=F32: ctx.enter_context(nc.sbuf_tensor(n, s, d))
        sem = semaphores(k, ctx)
        attr3 = sb("attr3", [P, k.TC + 1, 3])
        rows = [sb(f"rows{h}", [P, C, ROW]) for h in range(2)]
        to = [sb(f"to{h}", [P, 2, C], I32) for h in range(2)]
        loaded = sem("attr3_in")
        attr_in = [sem(f"attr32_in{h}") for h in range(2)]
        packed, free, put, cleared = sem("packed"), sem("rows_free"), sem("placed"), sem("rows_cleared")
        sent = k.sent
        started = sem("scatter_started")
        block = ctx.enter_context(nc.Block())
        main = a["edge_attr_32"][0:k.TC * P, :].rearrange("(p t) f -> p t f", p=P)
        EACH = 2 * C * 16

        @block.sync
        def _(sp):
            sp.dma_start(attr3[:, 0:k.TC, :], a["edge_attr_3"][0:k.TC * P, :].rearrange("(p t) f -> p t f", p=P)).then_inc(loaded, 16)
            sp.dma_start(attr3[0:k.REM, k.TC, :], a["edge_attr_3"][k.TC * P:k.E, :]).then_inc(loaded, 16)
            sp.wait_ge(cleared, 2)
            with sp.Fori(0, turns) as i:
                for h in range(2):
                    sp.wait_ge(free, 2 * i + h + 1)
                    sp.dma_start(rows[h][:, :, W_A32:W_A32 + D],
                                 main[:, bass.ds(i * (2 * C) + h * C, C), :]).then_inc(attr_in[h], 16)
            sp.wait_ge(free, 2 * turns + 1)
            sp.dma_start(rows[0][0:k.REM, 0, W_A32:W_A32 + D], a["edge_attr_32"][k.TC * P:k.E, :]).then_inc(attr_in[0], 16)

        @block.vector
        def _(dve):
            v = nc.vector
            for h in range(2):
                v.memset(rows[h][:, :, :], 0.0).then_inc(cleared, 1)
            dve.wait_ge(cleared, 2)
            dve.wait_ge(loaded, 32)

            def pack(h, at, n, parts=P):
                v.tensor_copy(rows[h][0:parts, 0:n, 0:4], k.words[0:parts, at, :])
                v.tensor_copy(rows[h][0:parts, 0:n, W_A3:W_A3 + 3], attr3[0:parts, at, :])
                v.tensor_copy(to[h][0:parts, :, 0:n], k.place[0:parts, :, at]).then_inc(packed, 1)

            with dve.Fori(0, turns) as i:
                for h in range(2):
                    dve.wait_ge(free, 2 * i + h + 1)
                    pack(h, bass.ds(i * (2 * C) + h * C, C), C)
            dve.wait_ge(free, 2 * turns + 1)
            pack(0, slice(k.TC, k.TC + 1), 1, k.REM)

        @block.gpsimd
        def _(pool):
            g = nc.gpsimd

            def scatter(h, n, parts=P):
                for u in range(n):
                    for s in range(2):
                        g.indirect_dma_start(k.edges[s], bass.IndirectOffsetOnAxis(ap=to[h][0:parts, s, u:u + 1], axis=0),
                                             rows[h][0:parts, u, :], None).then_inc(sent[h], 16)

            with pool.Fori(0, turns) as i:
                for h in range(2):
                    pool.wait_ge(packed, 2 * i + h + 1)
                    pool.wait_ge(attr_in[h], 16 * i + 16)
                    pool.sem_inc(started, 1)
                    scatter(h, C)
            pool.wait_ge(packed, 2 * turns + 1)
            pool.wait_ge(attr_in[0], 16 * turns + 16)
            scatter(0, 1, k.REM)
            pool.wait_ge(sent[0], EACH * turns + 32)

        @block.scalar
        def _(act):
            act.sem_inc(free, 2)
            with act.Fori(0, turns) as i:
                for h in range(2):
                    act.wait_ge(sent[h], EACH * i + EACH)
                    act.sem_inc(free, 1)


def read_sorted(k):
    nc = k.nc
    C = k.NT // Q // Q
    with ExitStack() as ctx:
        sb = lambda n, s, d=F32: ctx.enter_context(nc.sbuf_tensor(n, s, d))
        sem = semaphores(k, ctx)
        rows = [[sb(f"sorted{s}{h}", [P, C, ROW]) for h in range(2)] for s in range(2)]
        vec = sb("vec", [P, C, 3])
        sq = sb("vec_sq", [P, C, 3])
        cross = sb("vec_cross", [P, C, 3])
        t = sb("harm_t", [P, C, 6])
        harm = [sb(f"harm{h}", [P, C, NY]) for h in range(2)]
        rows_in = [sem(f"sorted_in{h}") for h in range(2)]
        squared, rooted = sem("vec_squared"), sem("vec_rooted")
        used, steps, made, stored = sem("sorted_used"), sem("read_steps"), sem("harm_made"), sem("harm_stored")
        n = k.NT // C
        view = [k.edges[s].rearrange("(p t) w -> p t w", p=P) for s in range(2)]
        K = 8
        block = ctx.enter_context(nc.Block())

        @block.sync
        def _(sp):
            with sp.Fori(0, n // 2) as i:
                for h in range(2):
                    sp.wait_ge(used, 2 * i + h + 1)
                    for s in range(2):
                        sp.dma_start(rows[s][h][:, :, :], view[s][:, bass.ds((2 * i + h) * C, C), :]).then_inc(rows_in[h], 16)

        @block.scalar
        def _(act):
            with act.Fori(0, n // 2) as i:
                for h in range(2):
                    act.wait_ge(squared, 2 * i + h + 1)
                    nc.scalar.activation(t[:, :, 0], t[:, :, 0], ACT.Sqrt).then_inc(rooted, 1)
                    act.wait_ge(made, 2 * i + h + 1)
                    act.dma_start(k.harm_dram.rearrange("p (t j) -> p t j", j=NY)[:, bass.ds((2 * i + h) * C, C), :],
                                  harm[h][:, :, :]).then_inc(stored, 16)
                    act.wait_ge(stored, (2 * i + h + 3) * 16)

        @block.vector
        def _(dve):
            v = nc.vector
            dve.sem_inc(used, 2)
            dve.sem_inc(stored, 32)
            with dve.Fori(0, n // 2) as i:
                for h in range(2):
                    c = 2 * i + h
                    step = Steps(dve, steps, c * K)
                    at = bass.ds(c * C, C)
                    dve.wait_ge(rows_in[h], 32 * i + 32)
                    r = rows[0][h]
                    v.tensor_copy(k.other[0][:, at], r[:, :, W_DST])
                    step(v.tensor_scalar(k.neglo[0][:, at], r[:, :, W_SLO], -1.0, None, ALU.mult))
                    r = rows[1][h]
                    v.tensor_copy(k.other[1][:, at], r[:, :, W_SRC])
                    step(v.tensor_scalar(k.neglo[1][:, at], r[:, :, W_DLO], -1.0, None, ALU.mult))
                    raw = r[:, :, W_A3:W_A3 + 3]
                    step(v.tensor_tensor(sq[:, :, :], raw, raw, ALU.mult))
                    step(v.tensor_reduce(t[:, :, 0], sq[:, :, :], AXX, ALU.add))
                    v.tensor_scalar(t[:, :, 0], t[:, :, 0], 1e-24, None, ALU.max).then_inc(squared, 1)
                    dve.wait_ge(rooted, c + 1)
                    step(v.reciprocal(t[:, :, 0], t[:, :, 0]))
                    step(v.tensor_tensor(vec[:, :, :], raw, t[:, :, 0].unsqueeze(2).to_broadcast([P, C, 3]), ALU.mult))
                    dve.sem_inc(used, 1)
                    step(v.tensor_tensor(sq[:, :, :], vec[:, :, :], vec[:, :, :], ALU.mult))
                    x, y, z = (vec[:, :, j] for j in range(3))
                    x2, y2, z2 = (sq[:, :, j] for j in range(3))
                    xy, yz, xz = (cross[:, :, j] for j in range(3))
                    v.tensor_tensor(xy, x, y, ALU.mult)
                    v.tensor_tensor(yz, y, z, ALU.mult)
                    v.tensor_tensor(xz, x, z, ALU.mult)
                    v.tensor_tensor(t[:, :, 1], x2, y2, ALU.subtract)
                    v.scalar_tensor_tensor(t[:, :, 2], x2, 3.0, y2, ALU.mult, ALU.subtract)
                    v.tensor_scalar(t[:, :, 3], z2, 5.0, -1.0, ALU.mult, ALU.add)
                    v.tensor_scalar(t[:, :, 4], z2, 5.0, -3.0, ALU.mult, ALU.add)
                    step(v.scalar_tensor_tensor(t[:, :, 5], y2, -3.0, x2, ALU.mult, ALU.add))
                    dve.wait_ge(stored, 16 * c + 16)
                    o = lambda j: harm[h][:, :, j]
                    v.memset(o(0), 0.28209479177387814)
                    for j, w in ((1, y), (2, z), (3, x)):
                        v.tensor_scalar(o(j), w, 0.4886025119029199, None, ALU.mult)
                    for j, w in ((4, xy), (5, yz), (7, xz)):
                        v.tensor_scalar(o(j), w, 1.0925484305920792, None, ALU.mult)
                    v.tensor_scalar(o(6), z2, 3 * 0.31539156525252005, -0.31539156525252005, ALU.mult, ALU.add)
                    v.tensor_scalar(o(8), t[:, :, 1], 0.5462742152960396, None, ALU.mult)
                    for j, first, factor, second in ((9, t[:, :, 2], 0.5900435899266435, y),
                                                     (10, xy, 2.890611442640554, z),
                                                     (11, t[:, :, 3], 0.4570457994644658, y),
                                                     (12, t[:, :, 4], 0.3731763325901154, z),
                                                     (13, t[:, :, 3], 0.4570457994644658, x),
                                                     (14, t[:, :, 1], 1.445305721320277, z),
                                                     (15, t[:, :, 5], 0.5900435899266435, x)):
                        last = v.scalar_tensor_tensor(o(j), first, factor, second, ALU.mult, ALU.mult)
                    last.then_inc(made, 1)
                    dve.wait_ge(made, c + 1)
                    assert step.n == K


def project_nodes(k, name, src, rhs, width, sinks, sink, finish=None, store=None):
    nc, G = k.nc, k.G
    with ExitStack() as ctx:
        sb = lambda n, s, d=F32: ctx.enter_context(nc.sbuf_tensor(f"{name}_{n}", s, d))
        pb = lambda n, s: ctx.enter_context(nc.psum_tensor(f"{name}_{n}", s, F32))
        sem = semaphores(k, ctx, f"{name}_")
        group, flat = sb("group", [P, G, D]), sb("flat", [D, G * P])
        turned_ps, product = pb("turned_ps", [D, 1024]), pb("product", [P, 512])
        copied, turned, flattened = sem("copied"), sem("turned"), sem("flattened")
        multiplied, sunk, steps, stored = sem("multiplied"), sem("sunk"), sem("steps"), sem("stored")
        block = ctx.enter_context(nc.Block())

        @block.gpsimd
        def _(pool):
            with pool.Fori(0, k.NG) as g:
                pool.wait_ge(turned, g + 1)
                nc.gpsimd.tensor_copy(group[:, :, :], src[:, bass.ds(g * G, G), :]).then_inc(copied, 1)

        @block.tensor
        def _(pe):
            pe.sem_inc(turned, 1)
            with pe.Fori(0, k.NG) as g:
                pe.wait_ge(copied, g + 1)
                for j in range(G):
                    last = nc.tensor.transpose(turned_ps[:, j * P:(j + 1) * P], group[:, j, :], k.ident[:, :])
                last.then_inc(turned, 1)
                pe.wait_ge(flattened, g + 1)
                pe.wait_ge(sunk, g + 1)
                for j in range(G):
                    last = nc.tensor.matmul(product[:, j * width:(j + 1) * width], flat[:, j * P:(j + 1) * P],
                                            rhs, start=True, stop=True)
                last.then_inc(multiplied, 1)

        @block.scalar
        def _(act):
            act.sem_inc(multiplied, 1)
            with act.Fori(0, k.NG) as g:
                act.wait_ge(turned, g + 2)
                act.wait_ge(multiplied, g + 1)
                nc.scalar.activation(flat[:, :], turned_ps[:, 0:G * P], ACT.Copy).then_inc(flattened, 1)

        @block.vector
        def _(dve):
            step = Steps(dve, steps)
            dve.sem_inc(sunk, 1)
            taken = product[:, 0:G * width].rearrange("p (j w) -> p j w", w=width)
            with dve.Fori(0, k.NG) as g:
                dve.wait_ge(multiplied, g + 2)
                turn = step.turn(g, sinks)
                sink(nc.vector, turn, bass.ds(g * G, G), taken)
                assert turn.n == sinks
                dve.sem_inc(sunk, 1)
            step.skip(k.NG * sinks)
            if finish:
                finish(nc.vector, step)
            dve.sem_inc(stored, 1)

        @block.sync
        def _(sp):
            if store:
                sp.wait_ge(stored, 1)
                for to, what in store:
                    sp.dma_start(rows_of(to), what).then_inc(stored, 16)
                sp.wait_ge(stored, 1 + 16 * len(store))


def harmonic_table(k):
    nc, G = k.nc, k.G
    with ExitStack() as ctx:
        sb = lambda n, s, d=F32: ctx.enter_context(nc.sbuf_tensor(n, s, d))
        sem = semaphores(k, ctx)
        group, flat, wide = sb("t0_group", [P, G, D]), sb("t0_flat", [D, G * P]), sb("t0_wide", [P, 2, G, NY * D])
        turned_ps = ctx.enter_context(nc.psum_tensor("t0_turned", [D, 1024], F32))
        product = ctx.enter_context(nc.psum_tensor("t0_product", [P, 6, 512], F32))
        copied, turned, flattened = sem("t0_copied"), sem("t0_turned_s"), sem("t0_flattened")
        multiplied, taken, stored = sem("t0_multiplied"), sem("t0_taken"), sem("t0_stored")
        out = rows_of(k.harm_table)
        block = ctx.enter_context(nc.Block())

        @block.gpsimd
        def _(pool):
            with pool.Fori(0, k.NG) as g:
                pool.wait_ge(turned, g + 1)
                nc.gpsimd.tensor_copy(group[:, :, :], k.H[:, bass.ds(g * G, G), :]).then_inc(copied, 1)

        @block.tensor
        def _(pe):
            pe.sem_inc(turned, 1)
            pe.sem_inc(taken, 6)
            with pe.Fori(0, k.NG) as g:
                pe.wait_ge(copied, g + 1)
                for j in range(G):
                    last = nc.tensor.transpose(turned_ps[:, j * P:(j + 1) * P], group[:, j, :], k.ident[:, :])
                last.then_inc(turned, 1)
                pe.wait_ge(flattened, g + 1)
                for j in range(G):
                    pe.wait_ge(taken, g * G + j + (6 if j == 0 else 1))
                    nc.tensor.matmul(product[:, j % 6, :], flat[:, j * P:(j + 1) * P], k.w0[:, :],
                                     start=True, stop=True).then_inc(multiplied, 1)

        @block.scalar
        def _(act):
            with act.Fori(0, k.NG) as g:
                act.wait_ge(turned, g + 2)
                act.wait_ge(taken, g * G + 6)
                nc.scalar.activation(flat[:, :], turned_ps[:, 0:G * P], ACT.Copy).then_inc(flattened, 1)

        @block.vector
        def _(dve):
            dve.sem_inc(stored, 16)
            for g in range(k.NG):
                if g >= 1:
                    dve.wait_ge(stored, g * 16)
                for j in range(G):
                    dve.wait_ge(multiplied, g * G + j + 1)
                    nc.vector.tensor_copy(wide[:, g % 2, j, :], product[:, j % 6, :]).then_inc(taken, 1)

        @block.sync
        def _(sp):
            for g in range(k.NG):
                sp.wait_ge(taken, 6 + (g + 1) * G)
                sp.dma_start(out[:, g * G:(g + 1) * G, :], wide[:, g % 2, :, :]).then_inc(stored, 16)
                sp.wait_ge(stored, 16 * (g + 2))


def gather(k, pool, s, c, q, free, copied, started, index, table, into, landed, before=0):
    g = k.nc.gpsimd
    pool.wait_ge(free, c + (before + 1))
    g.tensor_copy(index[q][:, :], k.other[s][:, bass.ds(c * U, U)]).then_inc(copied, 1)
    pool.wait_ge(copied, c + (before + 1))
    pool.sem_inc(started, 1)
    for u in range(U):
        g.indirect_dma_start(into[q][:, u, :], None, table,
                             bass.IndirectOffsetOnAxis(ap=index[q][:, u:u + 1], axis=0)).then_inc(landed[q], 16)


def one_hot_away(k, s, c, hot, near):
    for u in range(U):
        last = k.nc.scalar.activation(hot[:, u, :], k.iota[:, :], ACT.Abs, bias=k.neglo[s][:, bass.ds(c * U + u, 1)])
    last.then_inc(near, 1)


def one_hot_of(k, hot):
    return k.nc.scalar.activation(hot[:, :, :], hot[:, :, :], ACT.Relu, bias=1.0, scale=-1.0)


def blocks_of(k, engine, s, c):
    return [engine.value_load(k.tile_block[0:1, s, bass.ds(c * U + (U + u), 1)], min_val=0, max_val=k.NB - 1)
            for u in range(U)]


def harmonic_layer(k):
    nc, s = k.nc, 1
    with ExitStack() as ctx:
        sb = lambda n, sh, d=F32: ctx.enter_context(nc.sbuf_tensor(n, sh, d))
        pb = lambda n, sh: ctx.enter_context(nc.psum_tensor(n, sh, F32))
        sem = semaphores(k, ctx)
        index = [sb(f"h_index{q}", [P, U], I32) for q in range(Q)]
        got = [sb(f"h_got{q}", [P, U, NY * D]) for q in range(Q)]
        harm = [sb(f"h_harm{q}", [P, U, NY]) for q in range(Q)]
        attr = [sb(f"h_attr{q}", [P, U, D]) for q in range(Q)]
        hot = [sb(f"h_hot{q}", [P, U, P]) for q in range(Q)]
        msg = [sb(f"h_msg{q}", [P, U, D]) for q in range(Q)]
        hidden = [sb(f"h_hidden{q}", [P, U * P]) for q in range(Q)]
        turned = [sb(f"h_turned{q}", [D, U * P]) for q in range(2)]
        product = [sb(f"h_product{h}", [P, U, NY * D]) for h in range(2)]
        big, small = sb("ln_big1", [P, k.NB, D]), sb("ln_small1", [P, 2, k.NB])
        sums = pb("h_sums", [P, 2048])
        turned_ps = [pb(f"h_turned_ps{h}", [D, U * P]) for h in range(2)]
        hidden_ps = [pb(f"h_hidden_ps{h}", [P, U * P]) for h in range(2)]
        free, copied, started = sem("h_free"), sem("h_copied"), sem("h_started")
        landed, base = k.landed, k.landed_base
        loaded = [sem(f"h_loaded{q}") for q in range(Q)]
        stored = [sem(f"h_stored{q}") for q in range(Q)]
        near, made, flipped, flat = sem("h_near"), sem("h_made"), sem("h_flipped"), sem("h_flat")
        hidden_done, hidden_made, multiplied, msg_made = sem("h_hid_done"), sem("h_hid_made"), sem("h_multiplied"), sem("h_msg_made")
        steps, squares_summed, scaled = sem("h_steps"), sem("squares_summed1"), sem("scaled1")
        rows = k.edges[s].rearrange("(p t) w -> p t w", p=P)
        block = ctx.enter_context(nc.Block())

        @block.sync
        def _(sp):
            with sp.Fori(0, k.TURNS) as i:
                for q in range(Q):
                    c = i * Q + q
                    sp.wait_ge(free, c + 1)
                    sp.dma_start(harm[q][:, :, :], k.harm_dram.rearrange("p (t j) -> p t j", j=NY)[:, bass.ds(c * U, U), :]).then_inc(loaded[q], 16)
                    sp.dma_start(attr[q][:, :, :], rows[:, bass.ds(c * U, U), W_A32:W_A32 + D]).then_inc(loaded[q], 16)

        @block.gpsimd
        def _(pool):
            with pool.Fori(0, k.TURNS) as i:
                for q in range(Q):
                    gather(k, pool, s, i * Q + q, q, free, copied, started, index, k.harm_table, got, landed)

        @block.scalar
        def _(act):
            for q in range(Q):
                act.sem_inc(stored[q], 16)
            with act.Fori(0, k.TURNS) as i:
                for q in range(Q):
                    c = i * Q + q
                    act.wait_ge(free, c + 1)
                    one_hot_away(k, s, c, hot[q], near)
                    act.wait_ge(flipped, c + 1)
                    nc.scalar.activation(turned[q % 2][:, :], turned_ps[q % 2][:, :], ACT.Copy).then_inc(flat, 1)
                    act.wait_ge(near, c + 1)
                    one_hot_of(k, hot[q]).then_inc(made, 1)
                    act.wait_ge(hidden_done, c + 1)
                    act.wait_ge(stored[q], 16 * i + 16)
                    nc.scalar.activation(hidden[q][:, :], hidden_ps[q % 2][:, :], ACT.Relu, bias=k.en1_b[:, 0:1]).then_inc(hidden_made, 1)
                    act.wait_ge(hidden_made, c + 1)
                    act.dma_start(k.hid_dram[:, bass.ds(c * (U * P), U * P)], hidden[q][:, :]).then_inc(stored[q], 16)
            for q in range(Q):
                act.wait_ge(stored[q], 16 * (k.TURNS + 1))
            layernorm_root(k, act, small, squares_summed, scaled)

        @block.tensor
        def _(pe):
            pe.sem_inc(free, Q)
            zero_psum(k, sums, 4, steps)
            with pe.Fori(0, k.TURNS) as i:
                for q in range(Q):
                    c = i * Q + q
                    at = blocks_of(k, pe, s, c)
                    pe.wait_ge(loaded[q], 32 * i + 32)
                    for u in range(U):
                        last = nc.tensor.transpose(turned_ps[q % 2][:, u * P:(u + 1) * P], attr[q][:, u, :], k.ident[:, :])
                    last.then_inc(flipped, 1)
                    pe.wait_ge(flat, c + 1)
                    nc.tensor.matmul(hidden_ps[q % 2][:, :], k.en1[:, :], turned[q % 2][:, :], start=True, stop=True).then_inc(hidden_done, 1)
                    pe.wait_ge(made, c + 1)
                    pe.wait_ge(msg_made, c + 3)
                    for u in range(U):
                        last = nc.tensor.matmul(sums[:, bass.ds(at[u] * D, D)], hot[q][:, u, :], msg[q][:, u, :],
                                                start=False, stop=True, skip_group_check=True)
                    last.then_inc(free, 1)

        @block.vector
        def _(dve):
            v = nc.vector
            dve.sem_inc(msg_made, 2)
            with dve.Fori(0, k.TURNS) as i:
                for q in range(Q):
                    c = i * Q + q
                    dve.wait_ge(msg_made, c + 1)
                    dve.wait_ge(landed[q], i * (16 * U) + (base + 16 * U))
                    dve.wait_ge(loaded[q], 32 * i + 32)
                    for u in range(U):
                        last = v.tensor_tensor(product[q % 2][:, u, :].rearrange("p (o j) -> p o j", j=NY),
                                               got[q][:, u, :].rearrange("p (o j) -> p o j", j=NY),
                                               harm[q][:, u, :].unsqueeze(1).to_broadcast([P, D, NY]), ALU.mult)
                    last.then_inc(multiplied, 1)
                    dve.wait_ge(multiplied, c + 1)
                    v.tensor_reduce(msg[q][:, :, :].rearrange("p u o -> p (u o)"),
                                    product[q % 2][:, :, :].rearrange("p u (o j) -> p (u o) j", j=NY), AXX, ALU.add).then_inc(msg_made, 1)
            dve.wait_ge(free, k.TURNS * Q + Q)
            step = Steps(dve, steps, 1)
            step(v.tensor_tensor(k.X[:, :, :], k.X[:, :, :], sums[:, 0:k.NB * D].rearrange("p (b f) -> p b f", f=D), ALU.add))
            step(v.tensor_tensor(k.X[:, :, :], k.X[:, :, :], k.b0[:, :].unsqueeze(1).to_broadcast([P, k.NB, D]), ALU.add))
            layernorm_relu(k, step, k.X, k.H, big, small, squares_summed, scaled)
    k.landed_base += 1 * k.TURNS * 16 * U


def attention_tables(k):
    nc = k.nc
    with ExitStack() as ctx:
        sb = lambda n, s, d=F32: ctx.enter_context(nc.sbuf_tensor(n, s, d))
        sem = semaphores(k, ctx)
        least = sb("at_least", [P, 2])
        table = sb("at_table", [P, k.NB, D + HEADS])
        moved = sb("at_moved", [P, k.NB, HEADS])
        row = sb("at_row", [1, 2])
        ps = ctx.enter_context(nc.psum_tensor("at_ps", [P, 512], F32))
        steps, ready, turned, reduced, spread_s, stored = (sem(f"at_{n}") for n in ("steps", "ready", "turned", "reduced", "spread", "stored"))
        half = k.scores[:, :, HEADS:2 * HEADS]
        block = ctx.enter_context(nc.Block())

        @block.vector
        def _(dve):
            v = nc.vector
            step = Steps(dve, steps)
            step(v.tensor_copy(table[:, :, 0:D], k.H[:, :, :]))
            step(v.tensor_copy(table[:, :, D:D + HEADS], half))
            step(v.tensor_copy(moved[:, :, :], half))
            v.tensor_reduce(least[:, 0:1], moved[:, :, :].rearrange("p b h -> p (b h)"), AXX, ALU.min).then_inc(ready, 1)
            dve.wait_ge(turned, 1)
            v.tensor_reduce(row[:, 0:1], ps[0:1, 0:P], AXX, ALU.min).then_inc(reduced, 1)
            dve.wait_ge(spread_s, 1)
            step(v.tensor_scalar(k.least[:, 0:1], ps[:, 256:257], -1.0, 1.0, ALU.mult, ALU.add))
            step(v.tensor_scalar(moved[:, :, :], moved[:, :, :], k.least[:, 0:1], None, ALU.add))
            step(v.memset(k.most[:, :, :], 0.0))
            dve.sem_inc(ready, 1)

        @block.tensor
        def _(pe):
            pe.wait_ge(ready, 1)
            nc.tensor.transpose(ps[0:1, 0:P], least[:, 0:1], k.ident[:, :]).then_inc(turned, 1)
            pe.wait_ge(reduced, 1)
            nc.tensor.matmul(ps[:, 256:257], k.ones[0:1, :], row[0:1, 0:1], start=True, stop=True).then_inc(spread_s, 1)

        @block.sync
        def _(sp):
            sp.wait_ge(ready, 2)
            sp.dma_start(rows_of(k.far_table), moved[:, :, :]).then_inc(stored, 16)
            sp.dma_start(rows_of(k.near_table), table[:, :, :]).then_inc(stored, 16)
            sp.wait_ge(stored, 32)


def attention_maxima(k):
    nc, s = k.nc, 0
    with ExitStack() as ctx:
        sb = lambda n, sh, d=F32: ctx.enter_context(nc.sbuf_tensor(n, sh, d))
        sem = semaphores(k, ctx)
        index = [sb(f"m_index{q}", [P, U], I32) for q in range(Q)]
        got = [sb(f"m_got{q}", [P, U, HEADS]) for q in range(Q)]
        hot = [sb(f"m_hot{q}", [P, U, P]) for q in range(Q)]
        diag = [sb(f"m_diag{h}", [P, U, HEADS, P]) for h in range(2)]
        best = [sb(f"m_best{h}", [P, U * HEADS]) for h in range(2)]
        spread_ps = [ctx.enter_context(nc.psum_tensor(f"m_spread{h}", [P, U, HEADS * P], F32)) for h in range(2)]
        free, copied, started = sem("m_free"), sem("m_copied"), sem("m_started")
        landed, base = k.landed, k.landed_base
        near, made, diag_made, spread_s, taken, kept = (sem(f"m_{n}") for n in ("near", "made", "diag_made", "spread", "taken", "kept"))
        block = ctx.enter_context(nc.Block())

        @block.gpsimd
        def _(pool):
            with pool.Fori(0, k.TURNS) as i:
                for q in range(Q):
                    gather(k, pool, s, i * Q + q, q, free, copied, started, index, k.far_table, got, landed)

        @block.scalar
        def _(act):
            with act.Fori(0, k.TURNS) as i:
                for q in range(Q):
                    c = i * Q + q
                    act.wait_ge(free, c + 1)
                    one_hot_away(k, s, c, hot[q], near)
                    act.wait_ge(near, c + 1)
                    one_hot_of(k, hot[q]).then_inc(made, 1)

        @block.tensor
        def _(pe):
            pe.sem_inc(free, Q)
            with pe.Fori(0, k.TURNS) as i:
                for q in range(Q):
                    c = i * Q + q
                    pe.wait_ge(made, c + 1)
                    pe.wait_ge(diag_made, c + 1)
                    pe.wait_ge(taken, c + 1)
                    for u in range(U):
                        last = nc.tensor.matmul(spread_ps[q % 2][:, u, :], hot[q][:, u, :],
                                                diag[q % 2][:, u, :, :].rearrange("p h e -> p (h e)"), start=True, stop=True)
                    last.then_inc(free, 1)

        @block.vector
        def _(dve):
            v = nc.vector

            def keep(i, q):
                c, half = i * Q + q, q % 2
                dve.wait_ge(free, c + 1 + Q)
                v.tensor_reduce(best[half][:, :], spread_ps[half][:, :, :].rearrange("p u (h e) -> p (u h) e", h=HEADS),
                                AXX, ALU.max).then_inc(taken, 1)
                at = blocks_of(k, dve, s, c)
                dve.wait_ge(taken, c + 3)
                for u in range(U):
                    to = k.most[:, bass.ds(at[u], 1), :].rearrange("p a h -> p (a h)")
                    v.tensor_tensor(to, to, best[half][:, u * HEADS:(u + 1) * HEADS], ALU.max).then_inc(kept, 1)
                    dve.wait_ge(kept, c * U + (u + 1))

            def turn(i, first=False):
                for q in range(Q):
                    dve.wait_ge(landed[q], i * (16 * U) + (base + 16 * U))
                    wide = [P, U * HEADS, P]
                    v.tensor_tensor(diag[q % 2][:, :, :, :].rearrange("p u h e -> p (u h) e"),
                                    k.ident[:, :].unsqueeze(1).to_broadcast(wide),
                                    got[q][:, :, :].rearrange("p u h -> p (u h)").unsqueeze(2).to_broadcast(wide),
                                    ALU.mult).then_inc(diag_made, 1)
                    if q >= 1 or not first:
                        keep(i, q - 1)

            dve.sem_inc(taken, 2)
            turn(0, first=True)
            with dve.Fori(1, k.TURNS) as i:
                turn(i)
            keep(k.TURNS - 1, Q - 1)
    k.landed_base += 1 * k.TURNS * 16 * U


def attention_scores(k):
    nc = k.nc
    with ExitStack() as ctx:
        steps = semaphores(k, ctx)("own_steps")
        own_t = ctx.enter_context(nc.sbuf_tensor("own_t", [P, k.NB, HEADS], F32))
        block = ctx.enter_context(nc.Block())

        @block.vector
        def _(dve):
            v = nc.vector
            step = Steps(dve, steps)
            wide = [P, k.NB, HEADS]
            step(v.tensor_scalar(k.own[:, :, 0:HEADS], k.scores[:, :, 0:HEADS], k.fcb[:, 0:1], None, ALU.add))
            step(v.tensor_scalar(own_t[:, :, :], k.most[:, :, :], k.least[:, 0:1], None, ALU.subtract))
            step(v.tensor_tensor(own_t[:, :, :], own_t[:, :, :], k.own[:, :, 0:HEADS], ALU.add))
            step(v.scalar_tensor_tensor(k.own[:, :, HEADS:2 * HEADS], own_t[:, :, :], 0.2, own_t[:, :, :], ALU.mult, ALU.max))
            step(v.memset(k.pooled[:, :, :], 0.0))


def attention_layer(k):
    nc, s, W = k.nc, 0, HEADS * D + HEADS
    with ExitStack() as ctx:
        sb = lambda n, sh, d=F32: ctx.enter_context(nc.sbuf_tensor(n, sh, d))
        pb = lambda n, sh: ctx.enter_context(nc.psum_tensor(n, sh, F32))
        sem = semaphores(k, ctx)
        index = [sb(f"a_index{q}", [P, U], I32) for q in range(Q)]
        got = [sb(f"a_got{q}", [P, U, D + HEADS]) for q in range(Q)]
        hot = [sb(f"a_hot{q}", [P, U, P]) for q in range(Q)]
        cold = [sb(f"a_cold{h}", [P, U, P]) for h in range(2)]
        score = sb("a_score", [P, 2, U, HEADS])
        load = [sb(f"a_load{q}", [P, U, W]) for q in range(Q)]
        turned_ps = [pb(f"a_turned_ps{h}", [P, U * P]) for h in range(2)]
        own_ps = [pb(f"a_own_ps{h}", [P, 512]) for h in range(2)]
        sums = [pb(f"a_sums{h}", [P, U, 256]) for h in range(2)]
        free, copied, started = sem("a_free"), sem("a_copied"), sem("a_started")
        landed, base = k.landed, k.landed_base
        near, made, turned, flat, owned, steps, summed = (
            sem(f"a_{n}") for n in ("near", "made", "turned", "flat", "owned", "steps", "summed"))
        scored, powered, loaded, added = (sem(f"a_{n}") for n in ("scored", "powered", "loaded", "added"))
        K = 4
        block = ctx.enter_context(nc.Block())

        @block.gpsimd
        def _(pool):
            with pool.Fori(0, k.TURNS) as i:
                for q in range(Q):
                    gather(k, pool, s, i * Q + q, q, free, copied, started, index, k.near_table, got, landed)

        @block.scalar
        def _(act):
            def power(i, q):
                act.wait_ge(scored, i * Q + (q + 1))
                nc.scalar.activation(load[q % Q][:, :, HEADS * D:W], score[:, q % 2, :, :], ACT.Exp).then_inc(powered, 1)

            def turn(i, first=False):
                for q in range(Q):
                    c = i * Q + q
                    act.wait_ge(free, c + 1)
                    one_hot_away(k, s, c, hot[q], near)
                    act.wait_ge(near, c + 1)
                    one_hot_of(k, hot[q]).then_inc(made, 1)
                    act.wait_ge(turned, c + 1)
                    nc.scalar.activation(cold[q % 2][:, :, :].rearrange("p u e -> p (u e)"), turned_ps[q % 2][:, :], ACT.Copy).then_inc(flat, 1)
                    if q >= 1 or not first:
                        power(i, q - 1)

            turn(0, first=True)
            with act.Fori(1, k.TURNS) as i:
                turn(i)
            power(k.TURNS - 1, Q - 1)

        @block.tensor
        def _(pe):
            def sum_up(i, q):
                pe.wait_ge(loaded, i * Q + (q + 1))
                pe.wait_ge(added, i * Q + (q + 1))
                for u in range(U):
                    last = nc.tensor.matmul(sums[q % 2][:, u, 0:W], hot[q % Q][:, u, :], load[q % Q][:, u, :], start=True, stop=True)
                last.then_inc(free, 1)

            def turn(i, first=False):
                for q in range(Q):
                    c = i * Q + q
                    pe.wait_ge(made, c + 1)
                    for u in range(U):
                        last = nc.tensor.transpose(turned_ps[q % 2][:, u * P:(u + 1) * P], hot[q][:, u, :], k.ident[:, :])
                    last.then_inc(turned, 1)
                    at = blocks_of(k, pe, s, c)
                    pe.wait_ge(flat, c + 1)
                    for u in range(U):
                        last = nc.tensor.matmul(own_ps[q % 2][:, u * 2 * HEADS:(u + 1) * 2 * HEADS], cold[q % 2][:, u, :],
                                                k.own[:, bass.ds(at[u], 1), :].rearrange("p a h -> p (a h)"), start=True, stop=True)
                    last.then_inc(owned, 1)
                    if q >= 1 or not first:
                        sum_up(i, q - 1)

            pe.sem_inc(free, Q)
            pe.sem_inc(added, 2)
            turn(0, first=True)
            with pe.Fori(1, k.TURNS) as i:
                turn(i)
            sum_up(k.TURNS - 1, Q - 1)

        @block.vector
        def _(dve):
            v = nc.vector

            def rate(i, q):
                c = i * Q + q
                step = Steps(dve, steps, c * K)
                dve.wait_ge(landed[q], i * (16 * U) + (base + 16 * U))
                dve.wait_ge(owned, c + 1)
                own = own_ps[q % 2][:, 0:U * 2 * HEADS].rearrange("p (u t h) -> p u t h", t=2, h=HEADS)
                z = score[:, q % 2, :, :]
                step(v.tensor_tensor(z, got[q][:, :, D:D + HEADS], own[:, :, 0, :], ALU.add))
                step(v.scalar_tensor_tensor(z, z, 0.2, z, ALU.mult, ALU.max))
                step(v.tensor_tensor(z, z, own[:, :, 1, :], ALU.subtract))
                step(v.tensor_scalar(z, z, 0.0, None, ALU.min))
                dve.sem_inc(scored, 1)

            def weigh(i, q):
                dve.wait_ge(powered, i * Q + (q + 1))
                p, f = load[q % Q], got[q % Q]
                for u in range(U):
                    wide = [P, HEADS, D]
                    last = v.tensor_tensor(p[:, u, 0:HEADS * D].rearrange("p (h f) -> p h f", h=HEADS),
                                           f[:, u, 0:D].unsqueeze(1).to_broadcast(wide),
                                           p[:, u, HEADS * D:W].unsqueeze(2).to_broadcast(wide), ALU.mult)
                last.then_inc(loaded, 1)

            def add(i, q):
                c = i * Q + q
                step = Steps(dve, summed, c * U)
                at = blocks_of(k, dve, s, c)
                dve.wait_ge(free, c + 1 + Q)
                for u in range(U):
                    to = k.pooled[:, bass.ds(at[u], 1), :].rearrange("p a w -> p (a w)")
                    step(v.tensor_tensor(to, to, sums[q % 2][:, u, 0:W], ALU.add))
                dve.sem_inc(added, 1)

            def turn(i, first=False):
                for q in range(Q):
                    rate(i, q)
                    if q >= 1 or not first:
                        weigh(i, q - 1)
                    if q >= 2 or not first:
                        add(i, q - 2)

            turn(0, first=True)
            with dve.Fori(1, k.TURNS) as i:
                turn(i)
            weigh(k.TURNS - 1, Q - 1)
            add(k.TURNS - 1, Q - 2)
            add(k.TURNS - 1, Q - 1)
    k.landed_base += 1 * k.TURNS * 16 * U


def attention_output(k):
    nc, G = k.nc, k.G
    with ExitStack() as ctx:
        sb = lambda n, s, d=F32: ctx.enter_context(nc.sbuf_tensor(n, s, d))
        sem = semaphores(k, ctx)
        share = sb("o_share", [P, k.NB, HEADS])
        group, flat = sb("o_group", [P, G, P]), sb("o_flat", [P, G * P])
        big, small = sb("ln_big2", [P, k.NB, D]), sb("ln_small2", [P, 2, k.NB])
        turned_ps = ctx.enter_context(nc.psum_tensor("o_turned", [P, 1024], F32))
        product = ctx.enter_context(nc.psum_tensor("o_product", [P, 512], F32))
        ready, turned, flattened, multiplied, steps = (sem(f"o_{n}") for n in ("ready", "turned_s", "flattened", "multiplied", "steps"))
        squares_summed, scaled = sem("squares_summed2"), sem("scaled2")
        K = G + 2
        block = ctx.enter_context(nc.Block())

        @block.vector
        def _(dve):
            v = nc.vector
            step = Steps(dve, steps)
            step(v.tensor_scalar(share[:, :, :], k.pooled[:, :, HEADS * D:HEADS * D + HEADS], 1e-30, float(HEADS), ALU.max, ALU.mult))
            step(v.reciprocal(share[:, :, :], share[:, :, :]))
            with dve.Fori(0, k.NG) as g:
                turn = step.turn(g, K)
                for j in range(G):
                    wide = [P, HEADS, D]
                    turn(v.tensor_tensor(group[:, j, :].rearrange("p (h f) -> p h f", h=HEADS),
                                         k.pooled[:, bass.ds(g * G + j, 1), 0:HEADS * D].rearrange("p a (h f) -> p (a h) f", h=HEADS),
                                         share[:, bass.ds(g * G + j, 1), :].rearrange("p a h -> p (a h)").unsqueeze(2).to_broadcast(wide), ALU.mult))
                dve.sem_inc(ready, 1)
                dve.wait_ge(multiplied, g + 1)
                x = k.X[:, bass.ds(g * G, G), :]
                turn(v.tensor_tensor(x, x, product[:, 0:G * D].rearrange("p (j f) -> p j f", f=D), ALU.add))
                turn(v.tensor_tensor(x, x, k.b1[:, :].unsqueeze(1).to_broadcast([P, G, D]), ALU.add))
                assert turn.n == K
            step.skip(K * k.NG)
            layernorm_relu(k, step, k.X, k.H, big, small, squares_summed, scaled)

        @block.tensor
        def _(pe):
            with pe.Fori(0, k.NG) as g:
                pe.wait_ge(ready, g + 1)
                for j in range(G):
                    last = nc.tensor.transpose(turned_ps[:, j * P:(j + 1) * P], group[:, j, :], k.ident[:, :])
                last.then_inc(turned, 1)
                pe.wait_ge(flattened, g + 1)
                for j in range(G):
                    last = nc.tensor.matmul(product[:, j * D:(j + 1) * D], flat[:, j * P:(j + 1) * P], k.w1[:, :], start=True, stop=True)
                last.then_inc(multiplied, 1)

        @block.scalar
        def _(act):
            with act.Fori(0, k.NG) as g:
                act.wait_ge(turned, g + 1)
                nc.scalar.activation(flat[:, :], turned_ps[:, 0:G * P], ACT.Copy).then_inc(flattened, 1)
            layernorm_root(k, act, small, squares_summed, scaled)


def node_networks(k):
    nc, G = k.nc, k.G
    half = G * P // 2
    with ExitStack() as ctx:
        sb = lambda n, s, d=F32: ctx.enter_context(nc.sbuf_tensor(n, s, d))
        sem = semaphores(k, ctx)
        group, flat = sb("n_group", [P, G, D]), sb("n_flat", [D, G * P])
        inner = sb("n_inner", [P, 2, G * P])
        second = sb("n_second", [P, k.NB, D])
        turned_ps = ctx.enter_context(nc.psum_tensor("n_turned", [D, 1024], F32))
        inner_ps = ctx.enter_context(nc.psum_tensor("n_inner_ps", [P, 2, 2, 512], F32))
        outer_ps = ctx.enter_context(nc.psum_tensor("n_outer_ps", [P, 2, 256], F32))
        copied, turned, flattened, first_done, first_made, second_done, steps, stored = (
            sem(f"n_{n}") for n in ("copied", "turned_s", "flattened", "first_done", "first_made", "second_done", "steps", "stored"))
        block = ctx.enter_context(nc.Block())

        @block.gpsimd
        def _(pool):
            with pool.Fori(0, k.NG) as g:
                pool.wait_ge(turned, g + 1)
                nc.gpsimd.tensor_copy(group[:, :, :], k.H[:, bass.ds(g * G, G), :]).then_inc(copied, 1)

        @block.tensor
        def _(pe):
            pe.sem_inc(turned, 1)
            pe.sem_inc(steps, 2)
            with pe.Fori(0, k.NG) as g:
                pe.wait_ge(copied, g + 1)
                for j in range(G):
                    last = nc.tensor.transpose(turned_ps[:, j * P:(j + 1) * P], group[:, j, :], k.ident[:, :])
                last.then_inc(turned, 1)
                pe.wait_ge(flattened, g + 1)
                for n in range(2):
                    for m in range(2):
                        last = nc.tensor.matmul(inner_ps[:, n, m, 0:half], k.w2in[:, n, :], flat[:, m * half:(m + 1) * half],
                                                start=True, stop=True)
                last.then_inc(first_done, 1)
                pe.wait_ge(first_made, g + 1)
                pe.wait_ge(steps, 2 * g + 2)
                for n in range(2):
                    for j in range(G):
                        last = nc.tensor.matmul(outer_ps[:, n, j * D:(j + 1) * D], inner[:, n, j * P:(j + 1) * P],
                                                k.w2out[:, n, :], start=True, stop=True)
                last.then_inc(second_done, 1)

        @block.scalar
        def _(act):
            with act.Fori(0, k.NG) as g:
                act.wait_ge(turned, g + 2)
                nc.scalar.activation(flat[:, :], turned_ps[:, 0:G * P], ACT.Copy).then_inc(flattened, 1)
                act.wait_ge(first_done, g + 1)
                for n in range(2):
                    last = nc.scalar.activation(inner[:, n, :].rearrange("p (m e) -> p m e", m=2), inner_ps[:, n, :, 0:half],
                                                ACT.Relu, bias=k.b2in[:, n:n + 1])
                last.then_inc(first_made, 1)

        @block.vector
        def _(dve):
            with dve.Fori(0, k.NG) as g:
                dve.wait_ge(second_done, g + 1)
                for n, to in enumerate((k.first, second)):
                    nc.vector.tensor_tensor(to[:, bass.ds(g * G, G), :], outer_ps[:, n, 0:G * D].rearrange("p (j f) -> p j f", f=D),
                                            k.b2out[:, n, :].unsqueeze(1).to_broadcast([P, G, D]), ALU.add).then_inc(steps, 1)

        @block.sync
        def _(sp):
            sp.wait_ge(steps, 2 * k.NG + 2)
            sp.dma_start(rows_of(k.second_table), second[:, :, :]).then_inc(stored, 16)
            sp.wait_ge(stored, 16)


def gating_layer(k):
    nc, W = k.nc, 2 * D
    with ExitStack() as ctx:
        sb = lambda n, sh, d=F32: ctx.enter_context(nc.sbuf_tensor(n, sh, d))
        sem = semaphores(k, ctx)
        index = [sb(f"g_index{q}", [P, U], I32) for q in range(Q)]
        got = [sb(f"g_got{q}", [P, U, D]) for q in range(Q)]
        attr = [sb(f"g_attr{q}", [P, U, D]) for q in range(Q)]
        hot = [sb(f"g_hot{q}", [P, U, P]) for q in range(Q)]
        load = [sb(f"g_load{q}", [P, U, W]) for q in range(Q)]
        big, small = sb("ln_big3", [P, k.NB, D]), sb("ln_small3", [P, 2, k.NB])
        gated, quotient = sb("g_gated", [P, k.NB, D]), sb("g_quotient", [P, k.NB, D])
        banks = (k.NB * W + 511) // 512
        sums = ctx.enter_context(nc.psum_tensor("g_sums", [P, banks * 512], F32))
        free, copied, started = sem("g_free"), sem("g_copied"), sem("g_started")
        landed, base = k.landed, k.landed_base
        loaded = [sem(f"g_loaded{q}") for q in range(Q)]
        near, made, squashed, gated_s, steps = (sem(f"g_{n}") for n in ("near", "made", "squashed", "gated_s", "steps"))
        norms = [(sem(f"squares_summed{n}"), sem(f"scaled{n}")) for n in (3, 4)]
        chunks = k.TURNS * Q
        block = ctx.enter_context(nc.Block())

        @block.sync
        def _(sp):
            for s in range(2):
                rows = k.edges[s].rearrange("(p t) w -> p t w", p=P)
                with sp.Fori(0, k.TURNS) as i:
                    for q in range(Q):
                        c = i * Q + q
                        sp.wait_ge(free, c + (s * chunks + 1))
                        sp.dma_start(attr[q][:, :, :], rows[:, bass.ds(c * U, U), W_A32:W_A32 + D]).then_inc(loaded[q], 16)

        @block.gpsimd
        def _(pool):
            for s in range(2):
                with pool.Fori(0, k.TURNS) as i:
                    for q in range(Q):
                        gather(k, pool, s, i * Q + q, q, free, copied, started, index, k.second_table, got, landed, s * chunks)

        @block.scalar
        def _(act):
            for s in range(2):
                with act.Fori(0, k.TURNS) as i:
                    for q in range(Q):
                        c = i * Q + q
                        act.wait_ge(free, c + (s * chunks + 1))
                        one_hot_away(k, s, c, hot[q], near)
                        act.wait_ge(loaded[q], i * 16 + (s * k.TURNS + 1) * 16)
                        nc.scalar.activation(load[q][:, :, 0:D], attr[q][:, :, :], ACT.Sigmoid).then_inc(squashed, 1)
                        act.wait_ge(near, c + (s * chunks + 1))
                        one_hot_of(k, hot[q]).then_inc(made, 1)
            for squares_summed, scaled in norms:
                layernorm_root(k, act, small, squares_summed, scaled)

        @block.tensor
        def _(pe):
            pe.sem_inc(free, Q)
            zero_psum(k, sums, banks, steps)
            for s in range(2):
                with pe.Fori(0, k.TURNS) as i:
                    for q in range(Q):
                        c = i * Q + q
                        at = blocks_of(k, pe, s, c)
                        pe.wait_ge(made, c + (s * chunks + 1))
                        pe.wait_ge(gated_s, c + (s * chunks + 1))
                        for u in range(U):
                            last = nc.tensor.matmul(sums[:, bass.ds(at[u] * W, W)], hot[q][:, u, :], load[q][:, u, :],
                                                    start=False, stop=True, skip_group_check=True)
                        last.then_inc(free, 1)

        @block.vector
        def _(dve):
            v = nc.vector
            for s in range(2):
                with dve.Fori(0, k.TURNS) as i:
                    for q in range(Q):
                        c = i * Q + q
                        dve.wait_ge(landed[q], i * (16 * U) + (base + (s * k.TURNS + 1) * 16 * U))
                        dve.wait_ge(squashed, c + (s * chunks + 1))
                        v.tensor_tensor(load[q][:, :, D:W], load[q][:, :, 0:D], got[q][:, :, :], ALU.mult).then_inc(gated_s, 1)
            dve.wait_ge(free, 2 * chunks + Q)
            step = Steps(dve, steps, 1)
            total = sums[:, 0:k.NB * W].rearrange("p (b t f) -> p b t f", t=2, f=D)
            step(v.tensor_scalar(quotient[:, :, :], total[:, :, 0, :], 1e-7, None, ALU.add))
            step(v.reciprocal(quotient[:, :, :], quotient[:, :, :]))
            step(v.tensor_tensor(quotient[:, :, :], quotient[:, :, :], total[:, :, 1, :], ALU.mult))
            step(v.tensor_tensor(quotient[:, :, :], quotient[:, :, :], k.first[:, :, :], ALU.add))
            layernorm_relu(k, step, quotient, gated, big, small, *norms[0])
            step(v.tensor_tensor(k.X[:, :, :], k.X[:, :, :], k.H[:, :, :], ALU.add))
            step(v.tensor_tensor(k.X[:, :, :], k.X[:, :, :], gated[:, :, :], ALU.add))
            layernorm_relu(k, step, k.X, k.H, big, small, *norms[1])
    k.landed_base += 2 * k.TURNS * 16 * U


def edge_conditioned_layer(k, out):
    nc, s, G = k.nc, 1, k.G
    chunks, tiles = k.TURNS * Q, k.TURNS * Q * U
    W = 2 * D
    with ExitStack() as ctx:
        sb = lambda n, sh, d=F32: ctx.enter_context(nc.sbuf_tensor(n, sh, d))
        sem = semaphores(k, ctx)
        index = [sb(f"e_index{q}", [P, U], I32) for q in range(Q)]
        got = [sb(f"e_got{q}", [P, U, W]) for q in range(Q)]
        hidden = [sb(f"e_hidden{q}", [P, U, P]) for q in range(Q)]
        hot = [sb(f"e_hot{q}", [P, U, P]) for q in range(Q)]
        msg = [sb(f"e_msg{q}", [P, U, D]) for q in range(Q)]
        product = [sb(f"e_product{h}", [P, U, D, D + 1]) for h in range(2)]
        table = sb("e_table", [P, k.NB, W])
        group, flat = sb("e_group", [P, G, D]), sb("e_flat", [D, G * P])
        both, both_flat = sb("e_both", [P, G, W]), sb("e_both_flat", [W, G * P])
        gates, fresh = sb("e_gates", [P, G, 4 * D]), sb("e_fresh", [P, G, D])
        edge_w = [ctx.enter_context(nc.psum_tensor(f"e_w{h}", [P, D * D], F32)) for h in range(2)]
        sums = ctx.enter_context(nc.psum_tensor("e_sums", [P, 2048], F32))
        free, copied, started = sem("e_free"), sem("e_copied"), sem("e_started")
        landed, base = k.landed_last, 0
        loaded = [sem(f"e_loaded{q}") for q in range(Q)]
        near, made, joined, w_made, multiplied, msg_made, blank = (
            sem(f"e_{n}") for n in ("near", "made", "joined", "w_made", "multiplied", "msg_made", "blank"))
        t_copied, t_turned, t_flat, t_done, t_taken, t_stored = (sem(f"et_{n}") for n in ("copied", "turned", "flat", "done", "taken", "stored"))
        r_ready, r_turned, r_flat, r_done, r_gated, r_squashed, r_fresh, r_tanh, r_steps = (
            sem(f"er_{n}") for n in ("ready", "turned", "flat", "done", "gated", "squashed", "fresh", "tanh", "steps"))
        passed = sem("e_passed")
        cleared, cleared_ps = sem("e_cleared"), sem("e_cleared_ps")
        RK = 7
        block = ctx.enter_context(nc.Block())
        n_out = out.shape[0]

        @block.sync
        def _(sp):
            with sp.Fori(0, STEPS) as r:
                sp.wait_ge(t_taken, (r + 1) * (k.NG + 1))
                sp.dma_start(rows_of(k.round_table), table[:, :, :]).then_inc(t_stored, 16)
                with sp.Fori(0, k.TURNS) as i:
                    for q in range(Q):
                        c = i * Q + q
                        sp.wait_ge(free, r * (chunks + 1) + c + 2)
                        sp.dma_start(hidden[q][:, :, :].rearrange("p u e -> p (u e)"),
                                     k.hid_dram[:, bass.ds(c * (U * P), U * P)]).then_inc(loaded[q], 16)
            sp.wait_ge(cleared, 2)
            sp.dma_start(rows_of(out[0:(k.NB - 1) * P, :]), k.X[:, 0:k.NB - 1, :]).then_inc(t_stored, 16)
            sp.dma_start(out[(k.NB - 1) * P:n_out, :], k.X[0:k.LASTN, k.NB - 1, :]).then_inc(t_stored, 16)
            sp.wait_ge(t_stored, 16 * (STEPS + 2))

        @block.gpsimd
        def _(pool):
            g_ = nc.gpsimd
            with pool.Fori(0, STEPS) as r:
                pool.wait_ge(free, r * (chunks + 1) + Q)
                pool.sem_inc(passed, 1)
                g_.memset(hot[Q - 1][:, :, :], 0.0).then_inc(blank, 1)
                with pool.Fori(0, k.NG) as g:
                    n = r * k.NG + g
                    pool.wait_ge(t_turned, n + 1)
                    pool.wait_ge(r_steps, r * (k.NG * RK) + 1)
                    g_.tensor_copy(group[:, :, :], k.H[:, bass.ds(g * G, G), :]).then_inc(t_copied, 1)
                pool.wait_ge(t_stored, r * 16 + 16)
                pool.sem_inc(passed, 1)
                with pool.Fori(0, k.TURNS) as i:
                    for q in range(Q):
                        c = i * Q + q
                        pool.wait_ge(free, r * (chunks + 1) + c + 2)
                        g_.tensor_copy(index[q][:, :], k.other[s][:, bass.ds(c * U, U)]).then_inc(copied, 1)
                        pool.wait_ge(copied, r * chunks + c + 1)
                        pool.sem_inc(started, 1)
                        for u in range(U):
                            g_.indirect_dma_start(got[q][:, u, :], None, k.round_table,
                                                  bass.IndirectOffsetOnAxis(ap=index[q][:, u:u + 1], axis=0)).then_inc(landed[q], 16)

        @block.scalar
        def _(act):
            a_ = nc.scalar
            act.sem_inc(made, 1)
            act.sem_inc(joined, 1)
            with act.Fori(0, STEPS) as r:
                with act.Fori(0, k.NG) as g:
                    n = r * k.NG + g
                    act.wait_ge(t_turned, n + 2)
                    a_.activation(flat[:, :], edge_w[0][0:D, 0:G * P], ACT.Copy).then_inc(t_flat, 1)
                with act.Fori(0, k.TURNS) as i:
                    for q in range(Q):
                        c = i * Q + q
                        act.wait_ge(free, r * (chunks + 1) + c + 2)
                        one_hot_away(k, s, c, hot[q], near)
                        act.wait_ge(near, r * chunks + c + 1)
                        one_hot_of(k, hot[q]).then_inc(made, 1)
                        act.wait_ge(landed[q], (r * k.TURNS + i) * (16 * U) + (base + 16 * U))
                        act.wait_ge(msg_made, r * (tiles + 1) + c * U + 1)
                        a_.activation(product[q % 2][:, :, :, D], got[q][:, :, D:W], ACT.Copy).then_inc(joined, 1)
                with act.Fori(0, k.NG) as g:
                    n = r * k.NG + g
                    act.wait_ge(r_turned, n + 1)
                    a_.activation(both_flat[:, :], edge_w[0][0:W, 0:G * P], ACT.Copy).then_inc(r_flat, 1)
                    act.wait_ge(r_gated, n + 1)
                    a_.activation(gates[:, :, 0:2 * D], gates[:, :, 0:2 * D], ACT.Sigmoid).then_inc(r_squashed, 1)
                    act.wait_ge(r_fresh, n + 1)
                    a_.activation(fresh[:, :, :], fresh[:, :, :], ACT.Tanh).then_inc(r_tanh, 1)

        @block.tensor
        def _(pe):
            t_ = nc.tensor

            def add_up(q, u, block_no):
                return t_.matmul(sums[:, bass.ds(block_no * D, D)], hot[q][:, u, :], msg[q][:, u, :],
                                 start=False, stop=True, skip_group_check=True)

            pe.sem_inc(free, Q)
            pe.sem_inc(t_turned, 1)
            with pe.Fori(0, STEPS) as r:
                with pe.Fori(0, k.NG) as g:
                    n = r * k.NG + g
                    pe.wait_ge(t_copied, n + 1)
                    for j in range(G):
                        last = t_.transpose(edge_w[0][0:D, j * P:(j + 1) * P], group[:, j, :], k.ident[:, :])
                    last.then_inc(t_turned, 1)
                    pe.wait_ge(t_flat, n + 1)
                    pe.wait_ge(t_taken, r * (k.NG + 1) + g + 1)
                    for j in range(G):
                        last = t_.matmul(edge_w[1][:, j * D:(j + 1) * D], flat[:, j * P:(j + 1) * P], k.en2_b[:, :], start=True, stop=True)
                    last.then_inc(t_done, 1)
                zero_psum(k, sums, 4, cleared_ps)
                pe.wait_ge(blank, r + 1)
                pe.wait_ge(t_taken, (r + 1) * (k.NG + 1))
                pe.sem_inc(passed, 1)
                with pe.Fori(0, k.TURNS) as i:
                    for q in range(Q):
                        c = i * Q + q
                        before = (q - 1) % Q
                        at = [pe.value_load(k.tile_block[0:1, s, bass.ds(c * U + u, 1)], min_val=0, max_val=k.NB - 1) for u in range(U)]
                        pe.wait_ge(loaded[q], (r * k.TURNS + i) * 16 + 16)
                        for u in range(U):
                            t = r * tiles + c * U + u
                            pe.wait_ge(multiplied, t + 1)
                            for m in range(2):
                                last = t_.matmul(edge_w[u % 2][:, m * 512:(m + 1) * 512], hidden[q][:, u, :],
                                                 k.w2[:, m * 512:(m + 1) * 512], start=True, stop=True)
                            last.then_inc(w_made, 1)
                            if u == 0:
                                pe.wait_ge(made, r * chunks + c + 1)
                            pe.wait_ge(msg_made, r * (tiles + 1) + c * U + (u + 2))
                            last = add_up(before, u, at[u])
                        last.then_inc(free, 1)
                at = [pe.value_load(k.tile_block[0:1, s, bass.ds(chunks * U + u, 1)], min_val=0, max_val=k.NB - 1) for u in range(U)]
                pe.wait_ge(made, (r + 1) * chunks + 1)
                for u in range(U):
                    pe.wait_ge(msg_made, (r + 1) * (tiles + 1) + (u + 1))
                    last = add_up(Q - 1, u, at[u])
                last.then_inc(free, 1)
                with pe.Fori(0, k.NG) as g:
                    n = r * k.NG + g
                    pe.wait_ge(r_ready, n + 1)
                    pe.sem_inc(passed, 1)
                    for j in range(G):
                        last = t_.transpose(edge_w[0][0:W, j * P:(j + 1) * P], both[:, j, :], k.ident[:, :])
                    last.then_inc(r_turned, 1)
                    pe.wait_ge(r_flat, n + 1)
                    for j in range(G):
                        last = t_.matmul(edge_w[1][:, j * P:(j + 1) * P], both_flat[:, j * P:(j + 1) * P], k.rgru[:, :], start=True, stop=True)
                    last.then_inc(r_done, 1)

        @block.vector
        def _(dve):
            v = nc.vector

            def sum_up(q, u):
                v.tensor_reduce(msg[q][:, u, :], product[q % 2][:, u, :, :], AXX, ALU.add).then_inc(msg_made, 1)

            v.memset(product[1][:, U - 1, :, :], 0.0).then_inc(cleared, 1)
            dve.wait_ge(cleared, 1)
            v.memset(msg[Q - 1][:, :, :], 0.0).then_inc(msg_made, U)
            dve.sem_inc(multiplied, 2)
            dve.sem_inc(r_steps, 1)
            with dve.Fori(0, STEPS) as r:
                dve.sem_inc(t_taken, 1)
                with dve.Fori(0, k.NG) as g:
                    n = r * k.NG + g
                    at = bass.ds(g * G, G)
                    dve.wait_ge(t_done, n + 1)
                    v.tensor_copy(table[:, at, D:W], edge_w[1][:, 0:G * D].rearrange("p (j f) -> p j f", f=D))
                    v.tensor_copy(table[:, at, 0:D], k.H[:, at, :]).then_inc(t_taken, 1)
                with dve.Fori(0, k.TURNS) as i:
                    for q in range(Q):
                        c = i * Q + q
                        dve.wait_ge(landed[q], (r * k.TURNS + i) * (16 * U) + (base + 16 * U))
                        dve.wait_ge(msg_made, r * (tiles + 1) + c * U + 1)
                        for u in range(U):
                            t = r * tiles + c * U + u
                            dve.wait_ge(w_made, t + 1)
                            v.tensor_tensor(product[q % 2][:, u, :, 0:D],
                                            edge_w[u % 2][:, :].rearrange("p (o i) -> p o i", i=D),
                                            got[q][:, u, 0:D].unsqueeze(1).to_broadcast([P, D, D]), ALU.mult).then_inc(multiplied, 1)
                            dve.wait_ge(multiplied, t + 2)
                            if u == 0:
                                dve.wait_ge(joined, r * chunks + c + 1)
                                sum_up((q - 1) % Q, U - 1)
                            else:
                                if u == 1:
                                    dve.wait_ge(joined, r * chunks + c + 2)
                                sum_up(q, u - 1)
                dve.wait_ge(multiplied, (r + 1) * tiles + 2)
                sum_up(Q - 1, U - 1)
                dve.wait_ge(free, (r + 1) * (chunks + 1) + Q)
                dve.sem_inc(passed, 1)
                with dve.Fori(0, k.NG) as g:
                    n = r * k.NG + g
                    step = Steps(dve, r_steps, n * RK + 1)
                    at = bass.ds(g * G, G)
                    wide = [P, G, D]
                    z = both[:, :, 0:D]
                    total = sums[:, bass.ds(g * (G * D), G * D)].rearrange("p (j f) -> p j f", f=D)
                    step(v.tensor_tensor(z, total, k.conv_b[:, :].unsqueeze(1).to_broadcast(wide), ALU.add))
                    step(v.tensor_scalar(z, z, 0.0, None, ALU.max))
                    v.tensor_copy(both[:, :, D:W], k.H[:, at, :]).then_inc(r_ready, 1)
                    dve.wait_ge(r_done, n + 1)
                    v.tensor_tensor(gates[:, :, :], edge_w[1][:, 0:G * P].rearrange("p (j f) -> p j f", f=P),
                                    k.gate_b[:, :].unsqueeze(1).to_broadcast([P, G, P]), ALU.add).then_inc(r_gated, 1)
                    dve.wait_ge(r_squashed, n + 1)
                    reset, update = gates[:, :, 0:D], gates[:, :, D:2 * D]
                    step(v.tensor_tensor(fresh[:, :, :], reset, gates[:, :, 3 * D:4 * D], ALU.mult))
                    step(v.tensor_tensor(fresh[:, :, :], fresh[:, :, :], gates[:, :, 2 * D:3 * D], ALU.add))
                    dve.sem_inc(r_fresh, 1)
                    dve.wait_ge(r_tanh, n + 1)
                    step(v.tensor_tensor(z, both[:, :, D:W], fresh[:, :, :], ALU.subtract))
                    step(v.tensor_tensor(z, z, update, ALU.mult))
                    step(v.tensor_tensor(k.H[:, at, :], z, fresh[:, :, :], ALU.add))
                    assert step.n == RK
            v.tensor_tensor(k.X[:, :, :], k.X[:, :, :], k.H[:, :, :], ALU.add).then_inc(cleared, 1)


def build(nc, a, out):
    k = shapes(a["x"].shape[0], a["src"].shape[0])
    k.nc = nc
    dram = lambda n, s, d=F32: nc.dram_tensor(n, s, d).ap()
    k.edges = [dram(f"edges_by_{n}", [P * k.NT, ROW]) for n in ("src", "dst")]
    k.harm_dram = dram("harmonics", [P, k.NT * NY])
    k.block_dram = dram("tile_blocks", [2, k.BC * P], I32)
    k.harm_table = dram("harmonic_table", [k.NP, NY * D])
    k.far_table = dram("far_table", [k.NP, HEADS])
    k.near_table = dram("near_table", [k.NP, D + HEADS])
    k.second_table = dram("second_table", [k.NP, D])
    k.round_table = dram("round_table", [k.NP, 2 * D])
    k.hid_dram = dram("edge_hidden", [EH, k.NT * P])
    with ExitStack() as ctx:
        sb = lambda n, s, d=F32: ctx.enter_context(nc.sbuf_tensor(n, s, d))
        k.X = sb("X", [P, k.NB, D])
        k.H = sb("H", [P, k.NB, D])
        k.iota, k.ident, k.ones, k.below = (sb(n, [P, P]) for n in ("iota", "ident", "ones", "below"))
        k.zeros = sb("zeros", [P, 512])
        k.w0, k.b0 = sb("w0", [D, NY * D]), sb("b0", [P, D])
        k.wa, k.w1, k.fcb, k.b1 = sb("wa", [D, 2 * HEADS]), sb("w1", [P, D]), sb("fcb", [P, 1]), sb("b1", [P, D])
        k.w2in, k.b2in = sb("w2in", [D, 2, 128]), sb("b2in", [128, 2])
        k.w2out, k.b2out = sb("w2out", [128, 2, D]), sb("b2out", [P, 2, D])
        k.lin, k.lin_b, k.en1, k.en1_b = sb("lin", [D, D]), sb("lin_b", [P, D]), sb("en1", [D, EH]), sb("en1_b", [EH, 1])
        k.w2, k.en2_b, k.conv_b = sb("w2", [EH, D * D]), sb("en2_b", [D, D]), sb("conv_b", [P, D])
        k.rgru, k.gate_b = sb("rgru", [2 * D, 4 * D]), sb("gate_b", [P, 4 * D])
        k.tile_block = sb("tile_block", [1, 2, U + k.BC * P], I32)
        k.landed = [ctx.enter_context(nc.semaphore(f"landed{q}")) for q in range(Q)]
        k.landed_last = [ctx.enter_context(nc.semaphore(f"landed_last{q}")) for q in range(Q)]
        k.sent = [ctx.enter_context(nc.semaphore(f"sent{h}")) for h in range(2)]
        k.landed_base = 0
        load_and_prepare(k, a)
        k.other = [sb(f"other{s}", [P, k.NT], I32) for s in range(2)]
        k.neglo = [sb(f"neglo{s}", [P, k.NT]) for s in range(2)]
        with ExitStack() as inner:
            k.words = inner.enter_context(nc.sbuf_tensor("words", [P, k.TC + 1, 4], F32))
            k.place = inner.enter_context(nc.sbuf_tensor("place", [P, 2, k.TC + 1], I32))
            place_edges(k, a)
            sort_edges(k, a)
        read_sorted(k)
        harmonic_table(k)
        harmonic_layer(k)
        with ExitStack() as inner:
            k.scores, k.most, k.own, k.pooled = (
                inner.enter_context(nc.sbuf_tensor(n, [P, k.NB, w], F32))
                for n, w in (("scores", 2 * HEADS), ("most", HEADS), ("own", 2 * HEADS), ("pooled", HEADS * D + HEADS)))
            k.least = inner.enter_context(nc.sbuf_tensor("least", [P, 1], F32))
            project_nodes(k, "sc", k.H, k.wa[:, :], 2 * HEADS, 1,
                          lambda v, step, g, product: step(v.tensor_copy(k.scores[:, g, :], product)))
            attention_tables(k)
            attention_maxima(k)
            attention_scores(k)
            attention_layer(k)
            attention_output(k)
        with ExitStack() as inner:
            k.first = inner.enter_context(nc.sbuf_tensor("first", [P, k.NB, D], F32))
            node_networks(k)
            gating_layer(k)
        def relu_of_sum(v, step, g, product):
            step(v.tensor_tensor(k.H[:, g, :], product, k.lin_b[:, :].unsqueeze(1).to_broadcast([P, k.G, D]), ALU.add))
            step(v.tensor_scalar(k.H[:, g, :], k.H[:, g, :], 0.0, None, ALU.max))
        project_nodes(k, "li", k.H, k.lin[:, :], D, 2, relu_of_sum)
        edge_conditioned_layer(k, out)


def kernel(**inputs):
    import numpy as np
    import concourse.bacc as bacc
    from concourse.bass_utils import run_bass_kernel_spmd

    nc = bacc.Bacc("TRN2", target_bir_lowering=False, num_devices=1)
    arrays = {name: np.ascontiguousarray(a) for name, a in inputs.items()}
    a = {name: nc.dram_tensor(name, x.shape, mybir.dt.from_np(x.dtype), kind="ExternalInput").ap()
         for name, x in arrays.items()}
    out = nc.dram_tensor("out", arrays["x"].shape, F32, kind="ExternalOutput").ap()
    build(nc, a, out)
    return run_bass_kernel_spmd(nc, [arrays], core_ids=[0]).results[0]["out"]
```
